# Optimizing a Trainium2 kernel written in Bass

```python
import numpy as np
import jax
import jax.numpy as jnp

def _softmax(x, axis=-1):
    return jax.nn.softmax(x, axis=axis)

def _gelu(x):
    return jax.nn.gelu(x, approximate=True)

def _silu(x):
    return jax.nn.silu(x)

def _sigmoid(x):
    return jax.nn.sigmoid(x)

def _layernorm(x, axis=-1, eps=1e-05):
    m = jnp.mean(x, axis=axis, keepdims=True)
    v = jnp.var(x, axis=axis, keepdims=True)
    return (x - m) / jnp.sqrt(v + eps)

def _scatter_add(tgt, idx, src, axis=0):
    return tgt.at[idx].add(src)

def _segment_sum(src, seg, n):
    return jax.ops.segment_sum(src, seg, n)
kernel_name = 'mk_hybrid_d2_jaxref_r8_23c0ad'

def setup_inputs(seed: int=0):
    np.random.seed(seed)
    _w = jnp.asarray

    def _L0_attn_a_setup():
        import jax, jax.numpy as jnp
        import numpy as np
        N_HEADS = 16
        HEAD_DIM = 64
        DIM = 128
        BATCH = 2
        SEQ = 256
        key = jax.random.key(seed)
        ks = jax.random.split(key, 6)
        hd = N_HEADS * HEAD_DIM
        scale_in = 1.0 / np.sqrt(DIM)
        scale_out = 1.0 / np.sqrt(hd)
        return {'x': jax.random.normal(ks[0], (BATCH, SEQ, DIM), dtype=jnp.float32), 'Wq': jax.random.normal(ks[1], (DIM, hd), dtype=jnp.float32) * scale_in, 'Wk': jax.random.normal(ks[2], (DIM, hd), dtype=jnp.float32) * scale_in, 'Wv': jax.random.normal(ks[3], (DIM, hd), dtype=jnp.float32) * scale_in, 'Wo': jax.random.normal(ks[4], (hd, DIM), dtype=jnp.float32) * scale_out, 'bo': jnp.zeros((DIM,), dtype=jnp.float32)}
    _L0_attn_a_in = _L0_attn_a_setup()

    def _L0_attn_b_setup():
        import jax, jax.numpy as jnp
        import numpy as np
        import math
        D_MODEL = 128
        NUM_HEADS = 16
        key = jax.random.key(seed)
        k1, k2, k3 = jax.random.split(key, 3)
        B, S = (2, 256)
        x = jax.random.normal(k1, (B, S, D_MODEL), dtype=jnp.float32)
        W_kqv = jax.random.normal(k2, (D_MODEL, 3 * D_MODEL), dtype=jnp.float32) * (1.0 / math.sqrt(D_MODEL))
        m = jax.random.normal(k3, (NUM_HEADS, 1, 1), dtype=jnp.float32)
        return {'x': x, 'W_kqv': W_kqv, 'm': m}
    _L0_attn_b_in = _L0_attn_b_setup()

    def _L0_ffn_setup():
        import jax, jax.numpy as jnp
        import numpy as np
        NUM_EXPERTS = 8
        EXPERT_CAPACITY = 2.0
        key = jax.random.key(seed)
        k1, k2, k3, k4 = jax.random.split(key, 4)
        B, T, C, H, E = (4, 512, 128, 512, NUM_EXPERTS)
        x = jax.random.normal(k1, (B, T, C), jnp.float32)
        gate_w = jax.random.normal(k2, (C, E), jnp.float32) * 0.02
        w1 = jax.random.normal(k3, (E, C, H), jnp.float32) * 0.02
        w2 = jax.random.normal(k4, (E, H, C), jnp.float32) * 0.02
        return {'x': x, 'gate_w': gate_w, 'w1': w1, 'w2': w2}
    _L0_ffn_in = _L0_ffn_setup()

    def _L1_attn_a_setup():
        import jax, jax.numpy as jnp
        import numpy as np
        B, S, E = (4, 256, 128)
        H, KVH = (16, 4)
        D = E // H
        QL, KVL = (64, 32)
        ROPE_BASE = 10000.0

        def _rope(x):
            d = x.shape[-1]
            inv_freq = 1.0 / ROPE_BASE ** (jnp.arange(0, d, 2, dtype=jnp.float32) / d)
            t = jnp.arange(x.shape[1], dtype=jnp.float32)
            freqs = jnp.outer(t, inv_freq)
            cos = jnp.cos(freqs)[None, :, None, :].astype(x.dtype)
            sin = jnp.sin(freqs)[None, :, None, :].astype(x.dtype)
            x1, x2 = (x[..., ::2], x[..., 1::2])
            r1 = x1 * cos - x2 * sin
            r2 = x1 * sin + x2 * cos
            return jnp.stack([r1, r2], axis=-1).reshape(x.shape)
        key = jax.random.key(seed)
        ks = jax.random.split(key, 7)
        s = 0.02
        return {'x': jax.random.normal(ks[0], (B, S, E), dtype=jnp.float32), 'Wqa': jax.random.normal(ks[1], (E, QL), dtype=jnp.float32) * s, 'Wqb': jax.random.normal(ks[2], (QL, E), dtype=jnp.float32) * s, 'Wkva': jax.random.normal(ks[3], (E, KVL), dtype=jnp.float32) * s, 'Wkvb': jax.random.normal(ks[4], (KVL, KVH * D * 2), dtype=jnp.float32) * s, 'Wout': jax.random.normal(ks[5], (E, E), dtype=jnp.float32) * s, 'bout': jax.random.normal(ks[6], (E,), dtype=jnp.float32) * s}
    _L1_attn_a_in = _L1_attn_a_setup()

    def _L1_attn_b_setup():
        import jax, jax.numpy as jnp
        import numpy as np
        B, S, D = (4, 512, 128)
        C = 8.0
        key = jax.random.key(seed)
        k_x, k_wa, k_wx, k_ba, k_bx, k_lam = jax.random.split(key, 6)
        x = jax.random.normal(k_x, (B, S, D), dtype=jnp.float32)
        std = 1.0 / np.sqrt(D)
        Wa = jax.random.normal(k_wa, (D, D), dtype=jnp.float32) * std
        Wx = jax.random.normal(k_wx, (D, D), dtype=jnp.float32) * std
        ba = jax.random.normal(k_ba, (D,), dtype=jnp.float32) * 0.02
        bx = jax.random.normal(k_bx, (D,), dtype=jnp.float32) * 0.02
        u = jax.random.uniform(k_lam, (D,), dtype=jnp.float32, minval=0.9, maxval=0.999)
        Lam = -jnp.log(jnp.power(u, -1.0 / C) - 1.0)
        return {'x': x, 'Wa': Wa, 'Wx': Wx, 'ba': ba, 'bx': bx, 'Lam': Lam}
    _L1_attn_b_in = _L1_attn_b_setup()

    def _L1_ffn_setup():
        import jax, jax.numpy as jnp
        import numpy as np
        B, N, C, H, REG = (1, 2309, 128, 16, 5)
        D = C // H
        key = jax.random.key(seed)
        k0, k1, k2, k3 = jax.random.split(key, 4)
        x = jax.random.normal(k0, (B, N, C), dtype=jnp.float32)
        g_info = jax.random.normal(k1, (12, 2, C), dtype=jnp.float32)
        W_qkv = jax.random.normal(k2, (C, 3 * C), dtype=jnp.float32) * 0.02
        W_proj = jax.random.normal(k3, (C, C), dtype=jnp.float32) * 0.02
        b_proj = jnp.zeros((C,), dtype=jnp.float32)
        return {'x': x, 'g_info': g_info, 'W_qkv': W_qkv, 'W_proj': W_proj, 'b_proj': b_proj}
    _L1_ffn_in = _L1_ffn_setup()
    _d = {'L0_attn_a_x': _L0_attn_a_in['x'], 'L0_attn_a_Wq': _L0_attn_a_in['Wq'], 'L0_attn_a_Wk': _L0_attn_a_in['Wk'], 'L0_attn_a_Wv': _L0_attn_a_in['Wv'], 'L0_attn_a_Wo': _L0_attn_a_in['Wo'], 'L0_attn_a_bo': _L0_attn_a_in['bo'], 'L0_attn_b_W_kqv': _L0_attn_b_in['W_kqv'], 'L0_attn_b_m': _L0_attn_b_in['m'], 'L0_ffn_gate_w': _L0_ffn_in['gate_w'], 'L0_ffn_w1': _L0_ffn_in['w1'], 'L0_ffn_w2': _L0_ffn_in['w2'], 'L1_attn_a_Wqa': _L1_attn_a_in['Wqa'], 'L1_attn_a_Wqb': _L1_attn_a_in['Wqb'], 'L1_attn_a_Wkva': _L1_attn_a_in['Wkva'], 'L1_attn_a_Wkvb': _L1_attn_a_in['Wkvb'], 'L1_attn_a_Wout': _L1_attn_a_in['Wout'], 'L1_attn_a_bout': _L1_attn_a_in['bout'], 'L1_attn_b_Wa': _L1_attn_b_in['Wa'], 'L1_attn_b_Wx': _L1_attn_b_in['Wx'], 'L1_attn_b_ba': _L1_attn_b_in['ba'], 'L1_attn_b_bx': _L1_attn_b_in['bx'], 'L1_attn_b_Lam': _L1_attn_b_in['Lam'], 'L1_ffn_g_info': _L1_ffn_in['g_info'], 'L1_ffn_W_qkv': _L1_ffn_in['W_qkv'], 'L1_ffn_W_proj': _L1_ffn_in['W_proj'], 'L1_ffn_b_proj': _L1_ffn_in['b_proj']}
    _x0 = _d['L0_attn_a_x']
    _d['L0_attn_a_x'] = jax.random.normal(jax.random.fold_in(jax.random.key(seed), 1), (16, 256, 128), dtype=_x0.dtype)
    del _x0
    return _d

def reference(L0_attn_a_x, L0_attn_a_Wq, L0_attn_a_Wk, L0_attn_a_Wv, L0_attn_a_Wo, L0_attn_a_bo, L0_attn_b_W_kqv, L0_attn_b_m, L0_ffn_gate_w, L0_ffn_w1, L0_ffn_w2, L1_attn_a_Wqa, L1_attn_a_Wqb, L1_attn_a_Wkva, L1_attn_a_Wkvb, L1_attn_a_Wout, L1_attn_a_bout, L1_attn_b_Wa, L1_attn_b_Wx, L1_attn_b_ba, L1_attn_b_bx, L1_attn_b_Lam, L1_ffn_g_info, L1_ffn_W_qkv, L1_ffn_W_proj, L1_ffn_b_proj):

    def _L0_attn_a_ref(x, Wq, Wk, Wv, Wo, bo):
        import jax, jax.numpy as jnp
        import numpy as np
        N_HEADS = 16
        HEAD_DIM = 64
        DIM = 128
        BATCH = 2
        SEQ = 256
        b, s, _ = x.shape
        q = (x @ Wq).reshape(b, s, N_HEADS, HEAD_DIM)
        k = (x @ Wk).reshape(b, s, N_HEADS, HEAD_DIM)
        v = (x @ Wv).reshape(b, s, N_HEADS, HEAD_DIM)
        dot = jnp.einsum('bihd,bkhd->bhik', q, k)
        w = jax.nn.softmax(dot / jnp.sqrt(jnp.float32(HEAD_DIM)), axis=-1)
        a = jnp.einsum('bhij,bjhd->bihd', w, v)
        a = a.reshape(b, s, N_HEADS * HEAD_DIM)
        return a @ Wo + bo

    def _L0_attn_b_ref(x, W_kqv, m):
        import jax, jax.numpy as jnp
        import numpy as np
        import math
        D_MODEL = 128
        NUM_HEADS = 16
        B, S, D = x.shape
        H = NUM_HEADS
        hd = D // H
        scale = math.sqrt(D)
        kqv = x @ W_kqv
        k, q, v = jnp.split(kqv, 3, axis=-1)
        q = q.reshape(B, S, H, hd)
        k = k.reshape(B, S, H, hd)
        v = v.reshape(B, S, H, hd)
        rel = (jnp.arange(S)[None, :] - jnp.arange(S)[:, None]).astype(x.dtype)
        bias = m[None, :, :, :] * rel[None, None, :, :]
        score = jnp.einsum('bqhd,bkhd->bhqk', q, k) / scale + bias
        causal = jnp.tril(jnp.ones((S, S), dtype=bool))
        score = jnp.where(causal[None, None, :, :], score, -jnp.inf)
        attn = jax.nn.softmax(score, axis=-1)
        out = jnp.einsum('bhqk,bkhd->bqhd', attn, v).reshape(B, S, D)
        return out

    def _L0_ffn_ref(x, gate_w, w1, w2):
        import jax, jax.numpy as jnp
        import numpy as np
        NUM_EXPERTS = 8
        EXPERT_CAPACITY = 2.0
        B, T, C = x.shape
        E = gate_w.shape[1]
        cap = int(EXPERT_CAPACITY * T / E)
        scores = jnp.einsum('BTC,CE->BTE', x, gate_w)
        probs = jax.nn.softmax(scores, axis=-1)
        probs_et = jnp.transpose(probs, (0, 2, 1))
        top_p, top_idx = jax.lax.top_k(probs_et, cap)
        xin = jnp.take_along_axis(x[:, None, :, :], top_idx[..., None], axis=2)
        h = jax.nn.gelu(jnp.einsum('BElC,ECH->BElH', xin, w1), approximate=False)
        y = jnp.einsum('BElH,EHC->BElC', h, w2)
        y = y * top_p[..., None]
        b_idx = jnp.arange(B)[:, None, None]
        out = jnp.zeros((B, T, C), x.dtype).at[b_idx, top_idx].add(y)
        return out

    def _L1_attn_a_ref(x, Wqa, Wqb, Wkva, Wkvb, Wout, bout):
        import jax, jax.numpy as jnp
        import numpy as np
        B, S, E = (4, 256, 128)
        H, KVH = (16, 4)
        D = E // H
        QL, KVL = (64, 32)
        ROPE_BASE = 10000.0

        def _rope(x):
            d = x.shape[-1]
            inv_freq = 1.0 / ROPE_BASE ** (jnp.arange(0, d, 2, dtype=jnp.float32) / d)
            t = jnp.arange(x.shape[1], dtype=jnp.float32)
            freqs = jnp.outer(t, inv_freq)
            cos = jnp.cos(freqs)[None, :, None, :].astype(x.dtype)
            sin = jnp.sin(freqs)[None, :, None, :].astype(x.dtype)
            x1, x2 = (x[..., ::2], x[..., 1::2])
            r1 = x1 * cos - x2 * sin
            r2 = x1 * sin + x2 * cos
            return jnp.stack([r1, r2], axis=-1).reshape(x.shape)
        b, s, _ = x.shape
        scale = D ** (-0.5)
        q = (x @ Wqa @ Wqb).reshape(b, s, H, D)
        kv = (x @ Wkva @ Wkvb).reshape(b, s, KVH, D, 2)
        k, v = (kv[..., 0], kv[..., 1])
        q = _rope(q)
        k = _rope(k)
        g = H // KVH
        k = jnp.repeat(k, g, axis=2)
        v = jnp.repeat(v, g, axis=2)
        scores = jnp.einsum('bqhd,bkhd->bhqk', q, k) * scale
        causal = jnp.triu(jnp.ones((s, s), dtype=bool), k=1)
        scores = jnp.where(causal[None, None], -jnp.inf, scores)
        w = jax.nn.softmax(scores, axis=-1)
        out = jnp.einsum('bhqk,bkhd->bqhd', w, v).reshape(b, s, E)
        return out @ Wout + bout

    def _L1_attn_b_ref(x, Wa, Wx, ba, bx, Lam):
        import jax, jax.numpy as jnp
        import numpy as np
        B, S, D = (4, 512, 128)
        C = 8.0
        rt = jax.nn.sigmoid(jnp.einsum('bsd,hd->bsh', x, Wa) + ba)
        it = jax.nn.sigmoid(jnp.einsum('bsd,hd->bsh', x, Wx) + bx)
        log_a = -C * jax.nn.softplus(-Lam) * rt
        a = jnp.exp(log_a)
        b = jnp.sqrt(1.0 - a * a) * (it * x)

        def step(h, ab):
            a_t, b_t = ab
            h = a_t * h + b_t
            return (h, h)
        h0 = jnp.zeros((x.shape[0], x.shape[2]), dtype=x.dtype)
        _, y = jax.lax.scan(step, h0, (jnp.swapaxes(a, 0, 1), jnp.swapaxes(b, 0, 1)))
        return jnp.swapaxes(y, 0, 1)

    def _L1_ffn_ref(x, g_info, W_qkv, W_proj, b_proj):
        import jax, jax.numpy as jnp
        import numpy as np
        B, N, C, H, REG = (1, 2309, 128, 16, 5)
        D = C // H
        Bx, Nx, Cx = x.shape
        scale = D ** (-0.5)
        qkv = (x @ W_qkv).reshape(Bx, Nx, 3, H, D)
        q, k, v = (qkv[:, :, 0], qkv[:, :, 1], qkv[:, :, 2])
        g_layer = g_info[0].reshape(-1, H, D)
        q_g = g_layer[0]
        q_pure = q[:, REG:]
        q_n = q_pure / jnp.linalg.norm(q_pure, axis=-1, keepdims=True)
        qg_n = q_g / jnp.linalg.norm(q_g, axis=-1, keepdims=True)
        sim = (qg_n[None, None] * q_n).sum(-1).mean(-1)
        sim = (sim - sim.min()) / (sim.max() - sim.min())
        pos = sim > 0.9
        logits = jnp.einsum('bqhd,bkhd->bhqk', q * scale, k)

        def masked_attn(tok_mask):
            key_mask = jnp.concatenate([jnp.ones((Bx, REG), bool), tok_mask], axis=1)
            l = jnp.where(key_mask[:, None, None, :], logits, -jnp.inf)
            a = jax.nn.softmax(l, axis=-1)
            return jnp.einsum('bhqk,bkhd->bqhd', a, v)
        x_pos = masked_attn(pos)
        x_neg = masked_attn(~pos)
        reg_out = (x_pos[:, :REG] + x_neg[:, :REG]) * 0.5
        tok_out = jnp.where(pos[:, :, None, None], x_pos[:, REG:], x_neg[:, REG:])
        out = jnp.concatenate([reg_out, tok_out], axis=1).reshape(Bx, Nx, Cx)
        return out @ W_proj + b_proj
    x = L0_attn_a_x
    x = x + _L0_attn_a_ref(_layernorm(x, axis=-1), L0_attn_a_Wq, L0_attn_a_Wk, L0_attn_a_Wv, L0_attn_a_Wo, L0_attn_a_bo)
    x = x + _L0_ffn_ref(_layernorm(x, axis=-1), L0_ffn_gate_w, L0_ffn_w1, L0_ffn_w2)
    x = x + _L0_attn_b_ref(_layernorm(x, axis=-1), L0_attn_b_W_kqv, L0_attn_b_m)
    x = x + _L0_ffn_ref(_layernorm(x, axis=-1), L0_ffn_gate_w, L0_ffn_w1, L0_ffn_w2)
    x = x + _L1_attn_a_ref(_layernorm(x, axis=-1), L1_attn_a_Wqa, L1_attn_a_Wqb, L1_attn_a_Wkva, L1_attn_a_Wkvb, L1_attn_a_Wout, L1_attn_a_bout)
    x = x + _L1_ffn_ref(_layernorm(x, axis=-1), L1_ffn_g_info, L1_ffn_W_qkv, L1_ffn_W_proj, L1_ffn_b_proj)
    x = x + _L1_attn_b_ref(_layernorm(x, axis=-1), L1_attn_b_Wa, L1_attn_b_Wx, L1_attn_b_ba, L1_attn_b_bx, L1_attn_b_Lam)
    x = x + _L1_ffn_ref(_layernorm(x, axis=-1), L1_ffn_g_info, L1_ffn_W_qkv, L1_ffn_W_proj, L1_ffn_b_proj)
    return x

_drawn_inputs = setup_inputs


def setup_inputs(seed=0):
    import zlib

    import numpy as np

    out = dict(_drawn_inputs(seed))
    spreads = {'L0_attn_a_bo': (0.0, 0.1), 'L1_ffn_b_proj': (0.0, 0.1)}
    factors = {'L0_ffn_gate_w': 4.39,
     'L0_ffn_w1': 3.772,
     'L0_ffn_w2': 3.543,
     'L1_attn_a_Wqa': 8.0,
     'L1_attn_a_Wqb': 8.0,
     'L1_attn_a_Wkva': 8.0,
     'L1_attn_a_Wkvb': 8.0,
     'L1_attn_a_Wout': 8.0,
     'L1_attn_b_ba': 37.965,
     'L1_attn_b_bx': 8.0,
     'L1_ffn_g_info': 64.0,
     'L1_attn_a_bout': 4.002}
    for name, (base, spread) in spreads.items():
        noise = np.random.default_rng([zlib.crc32(name.encode()), seed]).standard_normal(out[name].shape)
        drawn = base * np.exp(spread * noise) if base else spread * noise
        out[name] = jnp.asarray(drawn.astype(out[name].dtype))
    for name, factor in factors.items():
        out[name] = (out[name] * factor).astype(out[name].dtype)
    return out
```

```python
from contextlib import ExitStack

import concourse.bass as bass
from concourse import mybir

F32 = mybir.dt.float32
BF16 = mybir.dt.bfloat16
I32 = mybir.dt.int32
ALU = mybir.AluOpType
ACT = mybir.ActivationFunctionType
AX = mybir.AxisListType

P = 128
NB = 16
S = 256
NT = S // P
TILES = NB * NT
C = 128
H = 16
EPS = 1e-5
BIG = 1e30

D8 = C // H
PARTS = 6
STACK = 64
ROW_SHIFT = PARTS * D8
ROW_SLOPE = ROW_SHIFT + 3
ROW_QPOS = ROW_SLOPE + 3
ROW_MASK = ROW_SHIFT + 3


class Tally:

    def __init__(self, sem, batch):
        self.sem, self.batch = sem, batch
        self.base, self.k, self.turn = 0, 0, None

    def add(self, n=1):
        self.k += n
        return self.value()

    def value(self, back=0):
        at = self.base + self.k - back
        return at if self.turn is None else self.turn * (2 * self.batch) + at

    def enter(self, turn):
        self.base, self.k, self.turn = self.base + self.k, 0, turn

    def leave(self, turns):
        assert self.k == 2 * self.batch, (self.sem, self.k, 2 * self.batch)
        self.base, self.k, self.turn = self.base + turns * self.k, 0, None


def wait(eng, sem, value):
    if isinstance(value, int) and value <= 0:
        return
    eng.wait_ge(sem, value)


def batches(eng, tallies, step, units=NB):
    step(-1, 1, True, False, False)
    step(0, 0, True, True, False)
    turns = (units - 2) // 2
    with eng.Fori(0, turns) as i:
        for t in tallies:
            t.enter(i)
        step(i * 2 + 1, 1, True, True, True)
        step(i * 2 + 2, 0, True, True, True)
    for t in tallies:
        t.leave(turns)
    step(units - 1, 1, False, True, True)
    step(units, 0, False, False, True)


def deep_batches(eng, tallies, step, units=NB):
    step(-2, 0, "A")
    step(-1, 1, "AM")
    step(0, 0, "AMB")
    turns = (units - 4) // 2
    with eng.Fori(0, turns) as i:
        for t in tallies:
            t.enter(i)
        step(i * 2 + 1, 1, "AMBE")
        step(i * 2 + 2, 0, "AMBE")
    for t in tallies:
        t.leave(turns)
    step(units - 3, 1, "AMBE")
    step(units - 2, 0, "MBE")
    step(units - 1, 1, "BE")
    step(units, 0, "E")


class Chain:

    def __init__(self, eng, sem, batch=0, settled=None):
        self.eng, self.t, self.settled = eng, Tally(sem, batch), settled

    def done(self, ins):
        ins.then_inc(self.t.sem, 1)
        self.eng.wait_ge(self.t.sem, self.t.add())
        if self.settled is not None:
            self.eng.sem_inc(self.settled, 1)


def make_identity(pool, sem, chain, t):
    chain.done(pool.memset(t[:], 0.0))
    pool.affine_select(out=t[:], in_=t[:], compare_op=ALU.not_equal, fill=1.0, base=0,
                       pattern=[[-1, P]], channel_multiplier=1).then_inc(sem, 1)


def load(nc, K, loads):
    with ExitStack() as ctx:
        ctx.enter_context(nc.cleanup_on_exit())
        loaded = nc.alloc_semaphore(name="loaded")
        x_loaded = nc.alloc_semaphore(name="x_loaded")
        own = nc.alloc_semaphore(name="pool_own")
        stats = nc.alloc_semaphore(name="stats")
        block = ctx.enter_context(nc.Block("load"))
        parts = 4

        @block.sync
        def _(sp):
            for n in range(parts):
                tiles = slice(n * TILES // parts, (n + 1) * TILES // parts)
                sp.dma_start(K.X[:, tiles, :], K.x_in[:, tiles, :]).then_inc(x_loaded, 16)
            for dst, src in loads:
                sp.dma_start(dst, src).then_inc(loaded, 16)
            sp.wait_ge(loaded, 16 * len(loads))

        @block.gpsimd
        def _(pool):
            c = Chain(pool, own)

            def select(ap, compare, fill, base, pattern, channel):
                c.done(pool.affine_select(out=ap, in_=ap, compare_op=compare, fill=fill, base=base,
                                          pattern=pattern, channel_multiplier=channel))

            for t in (K.ident, K.ident16):
                c.done(pool.memset(t[:], 0.0))
                select(t[:], ALU.not_equal, 1.0, 0, [[-1, P]], 1)
            c.done(pool.memset(K.causal_kq[:], 0.0))
            select(K.causal_kq[:], ALU.is_ge, -BIG, 0, [[1, P]], -1)
            c.done(pool.memset(K.causal_qk[:], 0.0))
            select(K.causal_qk[:], ALU.is_ge, -BIG, 0, [[-1, P]], 1)
            c.done(pool.iota(K.position_i[:], pattern=[[P, NT]], base=0, channel_multiplier=1))
            c.done(pool.tensor_copy(K.position[:], K.position_i[:]))
            c.done(pool.memset(K.own_head[:], 1.0))
            select(K.own_head[:], ALU.is_ge, 0.0, 0, [[-D8, H], [0, K.REG]], 1)
            select(K.own_head[:], ALU.is_ge, 0.0, D8 - 1, [[D8, H], [0, K.REG]], -1)
            c.done(pool.memset(K.not_first[:], 0.0))
            select(K.not_first[:], ALU.not_equal, -BIG, -(ROW_MASK + 1), [[0, K.REG * H]], 1)

        @block.vector
        def _(dve):
            for n in range(parts):
                dve.wait_ge(x_loaded, 16 * (n + 1)) if n == parts - 1 else None
            for t in range(TILES):
                dve.bn_stats(K.moments[:, t, :], K.X[:, t, :]).then_inc(stats, 1)
            dve.wait_ge(stats, TILES)


def norm_stats(K, s):
    me, ve, mo, vo = (K.moments[:, :, i] for i in (1, 2, 4, 5))

    def on_vector(dve):
        own = s["stat_dve"]
        dve.tensor_tensor(K.mean[:], me, mo, ALU.add).then_inc(own, 1)
        dve.tensor_tensor(K.spread[:], me, mo, ALU.subtract).then_inc(own, 1)
        dve.tensor_tensor(K.var[:], ve, vo, ALU.add).then_inc(own, 1)
        dve.wait_ge(own, 3)
        dve.tensor_scalar(K.mean[:], K.mean[:], 0.5, None, ALU.mult).then_inc(own, 1)
        dve.scalar_tensor_tensor(K.spread[:], K.spread[:], 0.25, K.spread[:], ALU.mult, ALU.mult).then_inc(own, 1)
        dve.tensor_scalar(K.var[:], K.var[:], 1.0 / C, EPS, ALU.mult, ALU.add).then_inc(own, 1)
        dve.wait_ge(own, 6)
        dve.tensor_tensor(K.var[:], K.var[:], K.spread[:], ALU.add).then_inc(s["var_ready"], 1)
        dve.wait_ge(s["rstd_ready"], 1)
        dve.reciprocal(K.rstd[:], K.rstd[:]).then_inc(own, 1)
        dve.wait_ge(own, 7)
        dve.scalar_tensor_tensor(K.shift[:], K.mean[:], -1.0, K.rstd[:], ALU.mult, ALU.mult).then_inc(s["norm_ready"], 1)

    def on_scalar(act):
        act.wait_ge(s["var_ready"], 1)
        act.activation(K.rstd[:], K.var[:], ACT.Sqrt).then_inc(s["rstd_ready"], 1)

    return on_vector, on_scalar



NARROW_BANK = {"norm": (0,), "lowrank": (1,), "qk": (1, 0), "v": (1, 0), "kstack": (1, 0), "qstack": (1, 0),
               "qshift": (1, 0), "turn": (1, 1, 1, 1), "attn": (1,), "project": (0,),
               "reg_k": (1,), "reg_scores": (0,), "reg_turn": (1,), "reg_value": (0,)}


MAXIMA = {slot: 2 for slot in range(6, 14)}
QUADS = H // 4
AHEAD = 8


def narrow_schedule(kind, parts):
    at = {"A": {0: ["xn"], 1: ["norm"], 4: ["qk0", "high0"], 5: ["rest0", "mid0"], 7: ["qk1", "high1", "low0", "rest1", "mid1"],
                8: ["low1"]},
          "M": {0: ["kstack0"], 2: ["kstack1"], 3: ["qstack0"], 5 if kind == "rope" else 4: ["qstack1"], 10: ["v0"], 11: ["v1"], 13: ["split"],
                15: ["qshift0", "qshift1"]},
          "E": {0: ["take3"], 1: ["turn3"], 3: ["attn"], 8 if kind == "rope" else 6: ["project"]}}
    heads = iter(range(H))
    for slot, count in MAXIMA.items():
        at["M"][slot] = [f"max{next(heads)}" for _ in range(count)] + at["M"].get(slot, [])
    if kind == "rope":
        at["A"][2] = ["lowrank"]
    if kind == "group":
        at["M"][8].append("reg_k")
        at["M"][9].append("reg_scores")
        at["M"][12].append("reg_turn")
        at["M"][14] = ["reg_value"]
    products, pieces = {H: [f"value{QUADS - 1}"]}, []
    for g in range(QUADS - 1):
        for after, what in enumerate(("value", "take", "turn")):
            products[4 * g + 5 + after] = [f"{what}{g}"]
    for slot in range(H + 1):
        if "B" in parts and slot < H:
            pieces.append(f"score{slot}")
        for part in "AME":
            if part in parts:
                pieces += at[part].get(slot, [])
        if "B" in parts:
            pieces += products.get(slot, [])
    return [(p.rstrip("0123456789"), int(p[len(p.rstrip("0123456789")):] or 0)) for p in pieces]


def narrow_attention(nc, K, kind, name, W):
    causal = kind != "group"
    project = kind != "slope"
    KB = 4 if kind == "rope" else H // 2
    HK = 4 if kind == "rope" else H
    G = H // HK
    used = {p for p, _ in narrow_schedule(kind, "AMBE")}
    if not project:
        used -= {"attn", "project"}
    fills = [sum(b == m for p in used if p in NARROW_BANK for b in NARROW_BANK[p]) for m in range(2)]
    QK = 160 if kind == "rope" else 2 * C
    REG, RH = K.REG, K.REG * H

    with ExitStack() as ctx:
        ctx.enter_context(nc.cleanup_on_exit())
        def sb(n, shape, dt=F32):
            return ctx.enter_context(nc.sbuf_tensor(f"{name}_{n}", shape, dt))

        s = {n: nc.alloc_semaphore(name=f"{name}_{n}") for n in (
            "stat_dve", "var_ready", "rstd_ready", "norm_ready",
            "pool_set", "dve_set",
            "xn",
            "full0", "full1",
            "drained0", "drained1",
            "high", "rotated", "rested", "mid", "low",
            "waited", "stacks", "scores", "maxed", "dve_own", "shifted", "scored", "exps",
            "valued", "taken", "turned", "biased", "stats", "reg_kt", "reg_probs", "reg_own", "reg_out")}
        full, drained = [s["full0"], s["full1"]], [s["drained0"], s["drained1"]]

        xn = sb("xn", [P, 2, NT, C])
        xnt = sb("xnt", [P, 2, S])
        parts = sb("parts", [P, NT, 3, QK], BF16)
        rest = sb("rest", [P, NT, QK])
        qp = sb("qp", [P, 2, NT, H, STACK], BF16)
        kp = sb("kp", [P, 2, NT, 2 * KB, STACK], BF16)
        qs = sb("qs", [P, 2, H // 2, S], BF16)
        kz = sb("kz", [P, 2, KB, 2, S], BF16)
        va = sb("va", [P, 2, NT, HK, 32])
        vplain = sb("vplain", [P, 2, NT, C]) if kind == "group" else None
        mx = sb("mx", [P, 2, NT, H])
        mrest = sb("mrest", [P, NT, H])
        pr = sb("pr", [P, AHEAD, 2 * S])
        rc = sb("rc", [P, QUADS, NT * 4])
        ot = sb("ot", [P, 2, S])
        att = sb("att", [P, 2, NT, C])
        att_t = sb("att_t", [P, 2, S])
        if kind == "slope":
            slope = sb("slope", [P, NT, H])
            srest = sb("srest", [P, NT, H])
        if kind == "rope":
            lr = sb("lr", [96, 2, S])
            ra = sb("ra", [P, NT, QK])
            rb = sb("rb", [P, NT, QK])
            rot = sb("rot", [P, NT, QK])
        if kind == "group":
            kt = sb("kt", [P, S])
            qblk = sb("qblk", [P, RH])
            negmax = sb("negmax", [RH, 1])
            sums = sb("sums", [RH, 1])
            rsum = sb("rsum", [RH, 1])
            px = sb("px", [RH, S])
            pxn = sb("pxn", [RH, S])
            pxt = sb("pxt", [P, NT * RH])
            rblk = sb("rblk", [P, RH])
            reg = sb("reg", [P, 2, REG])

        Sb, Tb, Ob, Mb = K.Sb, K.Tb, K.Ob, K.Mb
        stat_dve, stat_act = norm_stats(K, s)
        block = ctx.enter_context(nc.Block(name))

        def schedule(parts):
            return [(w, i) for w, i in narrow_schedule(kind, parts) if w in used or w == "attn"]

        def q_of(par, h):
            return qs[:, par, h // 2, :]

        def k_of(par, h):
            return kz[:, par, h // (2 if G == 1 else G), h % 2, :]

        def fill_tallies():
            return [Tally(s["full0"], fills[0]), Tally(s["full1"], fills[1])]

        def bank_of(tallies, what, i):
            if what not in NARROW_BANK or what not in used:
                return None, None
            b = NARROW_BANK[what][i]
            return b, tallies[b].add()

        @block.tensor
        def _(pe):
            fill = fill_tallies()
            xn_t, stacks_t, maxed_t = Tally(s["xn"], 1), Tally(s["stacks"], NT), Tally(s["maxed"], H)
            shifted_t, exps_t, scored_t = Tally(s["shifted"], 1), Tally(s["exps"], H), Tally(s["scored"], H)
            taken_t, turn_t, probs_t = Tally(s["taken"], QUADS), Tally(s["taken"], QUADS), Tally(s["reg_probs"], 1)
            tallies = fill + [xn_t, stacks_t, maxed_t, shifted_t, exps_t, scored_t, taken_t, turn_t]
            if kind == "group":
                tallies.append(probs_t)

            def all_drained():
                for b in range(2):
                    wait(pe, drained[b], fill[b].value())

            def step(n, par, todo):
                nxt = 1 - par
                for what, i in schedule(todo):
                    b, filling = bank_of(fill, what, i)
                    if b is not None:
                        bank = Mb[b]
                        wait(pe, drained[b], fill[b].value(1))
                    if what == "norm":
                        pe.wait_ge(s["xn"], xn_t.add())
                        for t in range(NT):
                            ins = pe.transpose(bank[:, t * P:(t + 1) * P], xn[:, par, t, :], K.ident[:])
                        ins.then_inc(full[b], 1)
                    elif what == "lowrank":
                        wait(pe, drained[0], fill[0].value())
                        pe.matmul(bank[0:96, 0:S], W["a"], xnt[:, par, :], start=True, stop=True).then_inc(full[b], 1)
                    elif what == "qk" and kind == "rope":
                        if i == 0:
                            wait(pe, drained[0], fill[0].value())
                        cols = slice(i * P, (i + 1) * P)
                        halves = bank[:, 0:QK].rearrange("p (z c) -> p z c", z=2)
                        pe.matmul(halves[:, :, 0:64], lr[0:64, par, cols], W["qb"], start=True, stop=True)
                        pe.matmul(halves[:, :, 64:80], lr[64:96, par, cols], W["kvb"][:, 0:32], start=True,
                                  stop=True).then_inc(full[b], 1)
                    elif what == "qk":
                        if i == 0:
                            wait(pe, drained[0], fill[0].value())
                        pe.matmul(bank[:, 0:QK], xnt[:, par, i * P:(i + 1) * P], W["qk"], start=True,
                                  stop=True).then_inc(full[b], 1)
                    elif what == "v" and kind == "rope":
                        pe.matmul(bank[:, 0:32], lr[64:96, nxt, i * P:(i + 1) * P], W["kvb"][:, 32:64], start=True,
                                  stop=True).then_inc(full[b], 1)
                    elif what == "v":
                        pe.matmul(bank[:, 0:C], xnt[:, nxt, i * P:(i + 1) * P], W["v"], start=True,
                                  stop=True).then_inc(full[b], 1)
                    elif what in ("kstack", "qstack", "qshift"):
                        if what == "kstack":
                            pe.wait_ge(s["stacks"], stacks_t.add())
                        if what == "qshift" and i == 0:
                            pe.wait_ge(s["shifted"], shifted_t.add())
                        src, blocks = (kp, KB) if what == "kstack" else (qp, H // 2)
                        for j in range(blocks):
                            ins = pe.transpose(bank[:].bitcast(BF16)[:, j * P:(j + 1) * P],
                                               src[:, nxt, i, 2 * j:2 * j + 2, :].rearrange("p h r -> p (h r)"),
                                               K.ident16[:])
                        ins.then_inc(full[b], 1)
                    elif what == "max":
                        if i == 0:
                            all_drained()
                        wait(pe, s["maxed"], maxed_t.add() - 2)
                        q, k = q_of(nxt, i), k_of(nxt, i)
                        for t in range(NT):
                            keys = P * (t + 1) if causal else S
                            at = Sb[i % 2][:, t * P:t * P + keys] if causal else Sb[i % 2][:, t * S:(t + 1) * S]
                            ins = pe.matmul(at, q[:, t * P:(t + 1) * P], k[:, 0:keys], start=True, stop=not causal)
                            if causal:
                                ins = pe.matmul(at[:, keys - P:keys], K.ident16[:], K.causal_qk[:], start=False, stop=True)
                        ins.then_inc(s["scores"], 1)
                    elif what == "score":
                        if i == 0:
                            all_drained()
                        wait(pe, s["exps"], scored_t.add() - 2)
                        q, k = q_of(par, i), k_of(par, i)
                        for t in range(NT):
                            first = t * P if causal else 0
                            at = Tb[i % 2][:, t * S:t * S + S - first]
                            ins = pe.matmul(at, k[:, t * P:(t + 1) * P], q[:, first:S], start=True, stop=not causal)
                            if causal:
                                ins = pe.matmul(at[:, 0:P], K.ident16[:], K.causal_kq[:], start=False, stop=True)
                        ins.then_inc(s["scored"], 1)
                    elif what == "value":
                        wait(pe, s["taken"], taken_t.add() - 2)
                        pe.wait_ge(s["exps"], exps_t.add(4))
                        for kt_ in range(NT):
                            first = kt_ * P if causal else 0
                            for z in range(4):
                                h = 4 * i + z
                                ins = pe.matmul(Ob[i % 2][32 * z:32 * z + 32, first:S], va[:, par, kt_, h // G, :],
                                                pr[:, h % AHEAD, kt_ * S:kt_ * S + S - first],
                                                start=(kt_ == 0), stop=(kt_ == NT - 1))
                        ins.then_inc(s["valued"], 1)
                    elif what == "turn":
                        pe.wait_ge(s["taken"], turn_t.add())
                        for t in range(NT):
                            ins = pe.transpose(bank[:, t * P:(t + 1) * P], ot[:, i % 2, t * P:(t + 1) * P], K.ident[:])
                        ins.then_inc(full[b], 1)
                    elif what == "attn":
                        if project:
                            wait(pe, drained[b], fill[b].value(1))
                            for t in range(NT):
                                ins = pe.transpose(bank[:, t * P:(t + 1) * P], att[:, nxt, t, :], K.ident[:])
                            ins.then_inc(full[b], 1)
                    elif what == "project":
                        wait(pe, drained[1], fill[1].value())
                        for t in range(NT):
                            ins = pe.matmul(bank[:, t * C:(t + 1) * C], att_t[:, nxt, t * P:(t + 1) * P],
                                            W["out"], start=True, stop=True)
                        ins.then_inc(full[b], 1)
                    elif what == "reg_k":
                        pe.matmul(bank[:, 0:S], W["k"], xnt[:, nxt, :], start=True, stop=True)
                        pe.matmul(bank[:, S:S + REG], W["q"], xnt[:, nxt, 0:REG], start=True, stop=True).then_inc(full[b], 1)
                    elif what == "reg_scores":
                        wait(pe, drained[1], fill[1].value())
                        pe.matmul(bank[0:RH, 0:S], qblk[:], kt[:], start=True, stop=False)
                        pe.matmul(bank[0:RH, 0:S], K.not_first[:], kz[0:STACK, nxt, 0, 0, :], start=False,
                                  stop=True).then_inc(full[b], 1)
                    elif what == "reg_turn":
                        pe.wait_ge(s["reg_probs"], probs_t.add())
                        for t in range(NT):
                            ins = pe.transpose(bank[:, t * RH:(t + 1) * RH], pxn[:, t * P:(t + 1) * P], K.ident[0:RH, 0:RH])
                        ins.then_inc(full[b], 1)
                    elif what == "reg_value":
                        wait(pe, drained[1], fill[1].value())
                        for t in range(NT):
                            ins = pe.matmul(bank[:, 0:RH], vplain[:, nxt, t, :], pxt[:, t * RH:(t + 1) * RH],
                                            start=(t == 0), stop=(t == NT - 1))
                        ins.then_inc(full[b], 1)

            pe.wait_ge(s["dve_set"], 1)
            deep_batches(pe, tallies, step)

        @block.scalar
        def _(act):
            fill = fill_tallies()
            scored_t, valued_t, stacks_t = Tally(s["scored"], H), Tally(s["valued"], QUADS), Tally(s["stacks"], NT)
            take_t = Tally(s["valued"], QUADS)
            negmax_t, regout_t = Tally(s["reg_own"], 4), Tally(s["reg_out"], 1)
            rotated_t, rested_t = Tally(s["rotated"], NT), Tally(s["rested"], NT)
            qk_filling = {}
            tallies = fill + [scored_t, valued_t, take_t, stacks_t] + ([negmax_t, regout_t] if kind == "group" else [])
            tallies += [rotated_t, rested_t] if kind == "rope" else []

            def step(n, par, todo):
                nxt = 1 - par
                for what, i in schedule(todo):
                    b, filling = bank_of(fill, what, i)
                    bank = None if b is None else Mb[b]
                    if what == "xn":
                        for t in range(NT):
                            tile = bass.ds((n + 2) * NT + t, 1)
                            ins = act.activation(xn[:, par, t, :], K.X[:, tile, :].rearrange("p a c -> p (a c)"),
                                                 ACT.Identity, bias=K.shift[:, tile], scale=K.rstd[:, tile])
                        ins.then_inc(s["xn"], 1)
                    elif what == "norm":
                        act.wait_ge(full[b], filling)
                        act.activation(xnt[:, par, :], bank[:, 0:S], ACT.Copy).then_inc(drained[b], 1)
                    elif what == "lowrank":
                        act.wait_ge(full[b], filling)
                        act.activation(lr[:, par, :], bank[0:96, 0:S], ACT.Copy).then_inc(drained[b], 1)
                    elif what == "qk":
                        qk_filling[i] = (b, filling)
                    elif what == "high":
                        b, filling = qk_filling[i]
                        wait(act, s["stacks"], stacks_t.add() - NT)
                        if kind == "rope":
                            act.wait_ge(s["rotated"], rotated_t.add())
                            act.activation(parts[:, i, 0, :], rot[:, i, :], ACT.Copy).then_inc(s["high"], 1)
                        else:
                            act.wait_ge(full[b], filling)
                            act.activation(parts[:, i, 0, :], Mb[b][:, 0:QK], ACT.Copy).then_inc(s["high"], 1)
                    elif what == "mid":
                        if kind == "rope":
                            act.wait_ge(s["rested"], rested_t.add())
                        else:
                            b, filling = qk_filling[i]
                            act.wait_ge(drained[b], filling)
                        act.activation(parts[:, i, 1, :], rest[:, i, :], ACT.Copy).then_inc(s["mid"], 1)
                    elif what == "v":
                        act.wait_ge(full[b], filling)
                        v = bank[:, 0:HK * D8]
                        if kind == "group":
                            act.activation(vplain[:, nxt, i, :], v, ACT.Copy)
                        act.activation(va[:, nxt, i, :, 0:D8], v.rearrange("p (h d) -> p h d", d=D8),
                                       ACT.Copy).then_inc(drained[b], 1)
                    elif what == "score":
                        act.wait_ge(s["scored"], scored_t.add())
                        if i % 4 == 0:
                            wait(act, s["valued"], valued_t.add() - AHEAD // 4)
                        cols = S + P if causal else 2 * S
                        act.activation(pr[:, i % AHEAD, 0:cols], Tb[i % 2][:, 0:cols], ACT.Exp).then_inc(s["exps"], 1)
                    elif what in ("qstack", "qshift") and i == 1:
                        act.wait_ge(full[b], filling)
                        act.activation(qs[:, nxt, :, i * P:(i + 1) * P],
                                       bank[:].bitcast(BF16).rearrange("p (j q) -> p j q", q=P), ACT.Copy).then_inc(drained[b], 1)
                    elif what == "take":
                        act.wait_ge(s["valued"], take_t.add())
                        act.activation(ot[:, i % 2, :], Ob[i % 2][:, 0:S], ACT.Copy).then_inc(s["taken"], 1)
                    elif what == "attn" and project:
                        act.wait_ge(full[b], filling)
                        first = 0
                        if kind == "group":
                            act.wait_ge(s["reg_out"], regout_t.add())
                            first = REG
                        act.activation(att_t[:, nxt, first:S], bank[:, first:S], ACT.Copy).then_inc(drained[b], 1)
                    elif what == "reg_k":
                        act.wait_ge(full[b], filling)
                        act.activation(kt[:], bank[:, 0:S], ACT.Copy).then_inc(s["reg_kt"], 1)
                    elif what == "reg_scores":
                        act.wait_ge(s["reg_own"], negmax_t.add())
                        negmax_t.add(3)
                        act.activation(px[:], bank[0:RH, 0:S], ACT.Exp, bias=negmax[:]).then_inc(drained[b], 1)
                    elif what == "reg_turn":
                        act.wait_ge(full[b], filling)
                        act.activation(pxt[:], bank[:, 0:NT * RH], ACT.Copy).then_inc(drained[b], 1)

            stat_act(act)
            act.wait_ge(s["norm_ready"], 1)
            act.wait_ge(s["pool_set"], K.narrow_sets[kind])
            act.wait_ge(s["dve_set"], 1)
            deep_batches(act, tallies, step)

        @block.vector
        def _(dve):
            fill = fill_tallies()
            high_t, scores_t = Tally(s["high"], NT), Tally(s["scores"], H)
            maxed_t, biased_t = Tally(s["maxed"], H), Tally(s["biased"], 1)
            own = Chain(dve, s["dve_own"], 3 + QUADS + (0 if project else 1))
            stats_t = Tally(s["stats"], NT)
            kt_t, reg_t = Tally(s["reg_kt"], 1), Tally(s["reg_own"], 4)
            mid_t = Tally(s["mid"], NT)
            qk_filling = {}
            tallies = fill + [scores_t, maxed_t, own.t, stats_t, high_t, mid_t]
            if project:
                tallies.append(biased_t)
            if kind == "group":
                tallies += [kt_t, reg_t]

            def step(n, par, todo):
                nxt = 1 - par
                for what, i in schedule(todo):
                    b, filling = bank_of(fill, what, i)
                    bank = None if b is None else Mb[b]
                    if what == "qk" and kind == "rope":
                        dve.wait_ge(full[b], filling)
                        wait(dve, s["high"], high_t.value() - NT + i + 1)
                        half = QK // 2
                        dve.tensor_tensor(ra[:, i, :], bank[:, 0:QK], K.cos[:, i, :], ALU.mult)
                        dve.tensor_tensor(rb[:, i, 0:half], bank[:, half:QK], K.sin[:, i, 0:half], ALU.mult)
                        dve.tensor_tensor(rb[:, i, half:QK], bank[:, 0:half], K.sin[:, i, half:QK],
                                          ALU.mult).then_inc(drained[b], 1)
                        dve.wait_ge(drained[b], filling)
                        dve.tensor_tensor(rot[:, i, :], ra[:, i, :], rb[:, i, :], ALU.add).then_inc(s["rotated"], 1)
                    elif what == "qk":
                        qk_filling[i] = (b, filling)
                    elif what == "rest":
                        dve.wait_ge(s["high"], high_t.add())
                        if kind == "rope":
                            dve.tensor_tensor(rest[:, i, :], rot[:, i, :], parts[:, i, 0, :],
                                              ALU.subtract).then_inc(s["rested"], 1)
                        else:
                            b, _ = qk_filling[i]
                            dve.tensor_tensor(rest[:, i, :], Mb[b][:, 0:QK], parts[:, i, 0, :],
                                              ALU.subtract).then_inc(drained[b], 1)
                    elif what == "low":
                        dve.wait_ge(s["mid"], mid_t.add())
                        dve.tensor_tensor(parts[:, i, 2, :], rest[:, i, :], parts[:, i, 1, :],
                                          ALU.subtract).then_inc(s["low"], 1)
                    elif what == "kstack":
                        dve.wait_ge(full[b], filling)
                        for z in range(2):
                            rows = slice(STACK * z, STACK * (z + 1))
                            ins = dve.tensor_copy(kz[rows, nxt, :, z, i * P:(i + 1) * P],
                                                  bank[rows].bitcast(BF16)[:, 0:KB * P].rearrange("p (j q) -> p j q", q=P))
                        ins.then_inc(drained[b], 1)
                    elif what in ("qstack", "qshift") and i == 0:
                        dve.wait_ge(full[b], filling)
                        dve.tensor_copy(qs[:, nxt, :, i * P:(i + 1) * P],
                                        bank[:].bitcast(BF16).rearrange("p (j q) -> p j q", q=P)).then_inc(drained[b], 1)
                    elif what == "max":
                        dve.wait_ge(s["scores"], scores_t.add())
                        maxed_t.add()
                        if causal:
                            dve.tensor_reduce(mx[:, nxt, 0, i:i + 1], Sb[i % 2][:, 0:P], AX.X, ALU.max, negate=True)
                            dve.tensor_reduce(mx[:, nxt, 1, i:i + 1], Sb[i % 2][:, P:P + S], AX.X, ALU.max,
                                              negate=True).then_inc(s["maxed"], 1)
                        else:
                            dve.tensor_reduce(mx[:, nxt, :, i], Sb[i % 2][:].rearrange("p (t k) -> p t k", k=S), AX.X,
                                              ALU.max, negate=True).then_inc(s["maxed"], 1)
                    elif what == "split":
                        to = [qp[:, nxt, :, :, ROW_SHIFT + j] for j in range(3)]
                        dve.wait_ge(s["maxed"], maxed_t.value())
                        own.done(dve.tensor_copy(to[0], mx[:, nxt]))
                        own.done(dve.tensor_tensor(mrest[:], mx[:, nxt], to[0], ALU.subtract))
                        own.done(dve.tensor_copy(to[1], mrest[:]))
                        dve.tensor_tensor(to[2], mrest[:], to[1], ALU.subtract).then_inc(s["shifted"], 1)
                    elif what == "turn":
                        dve.wait_ge(full[b], filling)
                        o = bank[:, 0:S].rearrange("p (t h e) -> p t h e", t=NT, e=32)
                        r = rc[:, i, :].rearrange("p (t h) -> p t h", t=NT)
                        own.done(dve.reciprocal(r, o[:, :, :, D8]))
                        to = att[:, nxt if i == QUADS - 1 else par, :, 4 * D8 * i:4 * D8 * (i + 1)]
                        dve.tensor_tensor(to.rearrange("p t (h d) -> p t h d", d=D8), o[:, :, :, 0:D8],
                                          r.unsqueeze(3).to_broadcast([P, NT, 4, D8]), ALU.mult).then_inc(drained[b], 1)
                        divided = (drained[b], filling)
                    elif what == "attn":
                        if not project:
                            dve.wait_ge(*divided)
                            x = K.X[:, bass.ds((n - 1) * NT, NT), :]
                            own.done(dve.tensor_tensor(x, x, att[:, nxt], ALU.add))
                            for t in range(NT):
                                dve.bn_stats(K.moments[:, bass.ds((n - 1) * NT + t, 1), :].rearrange("p a m -> p (a m)"),
                                             K.X[:, bass.ds((n - 1) * NT + t, 1), :].rearrange("p a c -> p (a c)")
                                             ).then_inc(s["stats"], 1)
                            stats_t.add(NT)
                        if kind == "group":
                            dve.wait_ge(full[b], filling)
                            dve.wait_ge(s["reg_own"], reg_t.value())
                            dve.scalar_tensor_tensor(att_t[:, nxt, 0:REG], bank[:, 0:REG], 0.5, reg[:, nxt, :],
                                                     ALU.mult, ALU.add).then_inc(s["reg_out"], 1)
                    elif what == "project":
                        dve.wait_ge(s["biased"], biased_t.add())
                        dve.wait_ge(full[b], filling)
                        x = K.X[:, bass.ds((n - 1) * NT, NT), :]
                        dve.tensor_tensor(x, x, bank[:, 0:NT * C].rearrange("p (t c) -> p t c", c=C),
                                          ALU.add).then_inc(drained[b], 1)
                        dve.wait_ge(drained[b], filling)
                        for t in range(NT):
                            dve.bn_stats(K.moments[:, bass.ds((n - 1) * NT + t, 1), :].rearrange("p a m -> p (a m)"),
                                         K.X[:, bass.ds((n - 1) * NT + t, 1), :].rearrange("p a c -> p (a c)")
                                         ).then_inc(s["stats"], 1)
                        stats_t.add(NT)
                    elif what == "reg_k":
                        dve.wait_ge(s["reg_kt"], kt_t.add())
                        q5 = bank[:, S:S + REG].unsqueeze(1).to_broadcast([P, H, REG])
                        dve.tensor_tensor(qblk[:].rearrange("p (h q) -> p h q", q=REG), q5,
                                          K.own_head[:].rearrange("p (h q) -> p h q", q=REG), ALU.mult).then_inc(drained[b], 1)
                    elif what == "reg_scores":
                        dve.wait_ge(full[b], filling)
                        dve.tensor_reduce(negmax[:], bank[0:RH, 0:S], AX.X, ALU.max, negate=True).then_inc(s["reg_own"], 1)
                        reg_t.add()
                        dve.wait_ge(drained[b], filling)
                        dve.tensor_reduce(sums[:], px[:], AX.X, ALU.add).then_inc(s["reg_own"], 1)
                        dve.wait_ge(s["reg_own"], reg_t.add())
                        dve.reciprocal(rsum[:], sums[:]).then_inc(s["reg_own"], 1)
                        dve.wait_ge(s["reg_own"], reg_t.add())
                        dve.tensor_scalar(pxn[:], px[:], rsum[:], 0.5, ALU.mult, ALU.mult).then_inc(s["reg_probs"], 1)
                    elif what == "reg_value":
                        dve.wait_ge(full[b], filling)
                        dve.tensor_tensor(rblk[:], bank[:, 0:RH], K.own_head[:], ALU.mult).then_inc(drained[b], 1)
                        dve.wait_ge(drained[b], filling)
                        dve.tensor_reduce(reg[:, nxt, :], rblk[:].rearrange("p (h q) -> p q h", q=REG), AX.X,
                                          ALU.add).then_inc(s["reg_own"], 1)
                        reg_t.add()

            stat_dve(dve)
            own.done(dve.memset(kz[:], 0.0))
            dve.wait_ge(s["pool_set"], K.narrow_sets[kind])
            if kind == "slope":
                m = K.slopes[:].unsqueeze(1).to_broadcast([P, NT, H])
                pos = K.position[:].unsqueeze(2).to_broadcast([P, NT, H])
                for row in (ROW_SLOPE, ROW_QPOS):
                    if row == ROW_SLOPE:
                        own.done(dve.tensor_copy(slope[:], m))
                    else:
                        own.done(dve.tensor_tensor(slope[:], m, pos, ALU.mult))
                        own.done(dve.tensor_scalar(slope[:], slope[:], -1.0, None, ALU.mult))
                    for par in range(2):
                        to = [qp[:, par, :, :, row + j] for j in range(3)]
                        own.done(dve.tensor_copy(to[0], slope[:]))
                        own.done(dve.tensor_tensor(srest[:], slope[:], to[0], ALU.subtract))
                        own.done(dve.tensor_copy(to[1], srest[:]))
                        own.done(dve.tensor_tensor(to[2], srest[:], to[1], ALU.subtract))
            if "scale" in W:
                own.done(dve.tensor_scalar(W["scale"][0], W["scale"][0], W["scale"][1], None, ALU.mult))
            dve.memset(mrest[:], 0.0).then_inc(s["dve_set"], 1)
            deep_batches(dve, tallies, step)
            dve.wait_ge(s["stats"], stats_t.value())

        @block.gpsimd
        def _(pool):
            fill = fill_tallies()
            xn_t = Tally(s["xn"], 1)
            stacks_t = Tally(s["stacks"], NT)
            low_t = Tally(s["low"], NT)

            def hold(sem, value):
                wait(pool, sem, value)
                pool.sem_inc(s["waited"], 1)
            tallies = fill + [stacks_t, low_t] + ([xn_t] if project else [])

            def step(n, par, todo):
                nxt = 1 - par
                for what, i in schedule(todo):
                    b, filling = bank_of(fill, what, i)
                    if what == "xn" and project:
                        hold(s["xn"], xn_t.add())
                        x = K.X[:, bass.ds((n + 2) * NT, NT), :]
                        pool.tensor_tensor(x, x, W["bias"].unsqueeze(1).to_broadcast([P, NT, C]),
                                           ALU.add).then_inc(s["biased"], 1)
                    elif what == "qk":
                        hold(s["low"], low_t.add())
                        if i == 0:
                            pool.memset(qp[:, par, :, :, ROW_SHIFT:ROW_SHIFT + 3], 0.0)
                            if kind == "group":
                                for st, m in ((qp, K.mask_q), (kp, K.mask_k)):
                                    for t in range(NT):
                                        tile = m[:, bass.ds((n + 2) * NT + t, 1), :]
                                        pool.tensor_copy(st[:, par, t, :, ROW_MASK:ROW_MASK + 2],
                                                         tile.to_broadcast([P, H, 2]))
                        if kind == "rope":
                            half = QK // 2
                            for z in range(2):
                                src = parts[:, i, :, z * half:(z + 1) * half]
                                q = src[:, :, 0:64].rearrange("p a (h d) -> p h a d", d=4)
                                for row, a, k in ((0, 0, 3), (3, 1, 2), (5, 2, 1)):
                                    for r in range(k):
                                        at = (row + r) * D8 + 4 * z
                                        pool.tensor_copy(qp[:, par, i, :, at:at + 4], q[:, :, a, :])
                                kk = src[:, :, 64:80].rearrange("p a (h d) -> p h a d", d=4)
                                for row, a in ((0, 0), (1, 1), (2, 2), (3, 0), (4, 1), (5, 0)):
                                    at = row * D8 + 4 * z
                                    ins = pool.tensor_copy(
                                        kp[:, par, i, :, at:at + 4].rearrange("p (h e) d -> p h e d", e=2),
                                        kk[:, :, a, :].unsqueeze(2).to_broadcast([P, HK, 2, 4]))
                        else:
                            q = parts[:, i, :, W["q_at"]:W["q_at"] + C].rearrange("p a (h d) -> p h a d", d=D8)
                            kk = parts[:, i, :, W["k_at"]:W["k_at"] + C].rearrange("p a (h d) -> p h a d", d=D8)
                            for row, a, k in ((0, 0, 3), (3, 1, 2), (5, 2, 1)):
                                pool.tensor_copy(qp[:, par, i, :, row * D8:(row + k) * D8].rearrange("p h (a d) -> p h a d", d=D8),
                                                 q[:, :, a:a + 1, :].to_broadcast([P, H, k, D8]))
                            for row, k in ((0, 3), (3, 2), (5, 1)):
                                ins = pool.tensor_copy(kp[:, par, i, :, row * D8:(row + k) * D8].rearrange("p h (a d) -> p h a d", d=D8),
                                                       kk[:, :, 0:k, :])
                        ins.then_inc(s["stacks"], 1)
                        stacks_t.add()

            done = 0
            for ap, value in [(qp[:], 0.0), (kp[:], 0.0), (va[:], 0.0)]:
                pool.memset(ap, value).then_inc(s["pool_set"], 1)
                done += 1
            pool.wait_ge(s["pool_set"], done)
            for ap, value in [(kp[:, :, :, :, ROW_SHIFT:ROW_SHIFT + 3], 1.0), (va[:, :, :, :, D8:D8 + 1], 1.0)] + (
                    [(kp[:, :, :, :, ROW_QPOS:ROW_QPOS + 3], 1.0)] if kind == "slope" else []):
                pool.memset(ap, value).then_inc(s["pool_set"], 1)
                done += 1
            if kind == "slope":
                for par in range(2):
                    for t in range(NT):
                        pos = K.position[:, t:t + 1].unsqueeze(2).to_broadcast([P, H, 3])
                        pool.tensor_copy(kp[:, par, t, :, ROW_SLOPE:ROW_SLOPE + 3], pos).then_inc(s["pool_set"], 1)
                        done += 1
            assert done == K.narrow_sets[kind]
            deep_batches(pool, tallies, step)


def groups(nc, K, name, W):
    REG = K.REG
    with ExitStack() as ctx:
        ctx.enter_context(nc.cleanup_on_exit())
        def sb(n, shape, dt=F32):
            return ctx.enter_context(nc.sbuf_tensor(f"{name}_g_{n}", shape, dt))

        s = {n: nc.alloc_semaphore(name=f"{name}_g_{n}") for n in (
            "stat_dve", "var_ready", "rstd_ready", "norm_ready", "xn", "turned", "xnt", "q_full", "q_read",
            "squared", "summed", "sums", "blocks", "own", "guided", "inv", "pool_own", "ends", "mm", "two", "spread", "all",
            "pos", "ready", "scaled")}
        xn = sb("xn", [P, 2, NT, C])
        xnt = sb("xnt", [P, 2, S])
        q = sb("q", [P, 2, S])
        square = sb("square", [P, 2, S])
        own_block, guide_block, g_column = sb("own_block", [P, H]), sb("guide_block", [P, H]), sb("g_column", [P, 1])
        g_sq, g_sum, g_inv, g_half = sb("g_sq", [P, C]), sb("g_sum", [P, H]), sb("g_inv", [P, H]), sb("g_half", [P, H])
        guide = sb("guide", [P, C])
        dots_squares, inv = sb("dots_squares", [P, TILES, 2, H]), sb("inv", [P, TILES, H])
        dots, squares = dots_squares[:, :, 0, :], dots_squares[:, :, 1, :]
        sim, low, top = sb("sim", [P, TILES]), sb("low", [P, TILES]), sb("top", [P, TILES])
        ends, two, diag, ones = sb("ends", [P, 2]), sb("two", [2, 1]), sb("diag", [2, 2]), sb("ones", [2, P])
        both, span, first = sb("both", [P, 2]), sb("span", [P, 1]), sb("first", [P, TILES])
        first_q, first_k, second_k, second = sb("first_q", [P, TILES]), sb("first_k", [P, TILES]), sb("second_k", [P, TILES]), sb("second", [P, TILES])
        stat_dve, stat_act = norm_stats(K, s)
        block = ctx.enter_context(nc.Block(name + "_g"))
        banks = K.banks
        turns = NB // 2

        @block.scalar
        def _(act):
            stat_act(act)
            act.wait_ge(s["norm_ready"], 1)

            def normed(n, par):
                for t in range(NT):
                    tile = bass.ds(n * NT + t, 1)
                    ins = act.activation(xn[:, par, t, :], K.X[:, tile, :].rearrange("p a c -> p (a c)"), ACT.Identity,
                                         bias=K.shift[:, tile], scale=K.rstd[:, tile])
                ins.then_inc(s["xn"], 1)

            def batch(n, par, count, more=True):
                act.wait_ge(s["turned"], count)
                act.activation(xnt[:, par, :], banks[par][:, 0:S], ACT.Copy).then_inc(s["xnt"], 1)
                if more:
                    normed(n + 2, par)
                act.wait_ge(s["q_full"], count)
                wait(act, s["summed"], count - 2)
                act.activation(q[:, par, :], banks[2 + par][:, 0:S], ACT.Copy).then_inc(s["q_read"], 1)
            normed(0, 0)
            normed(1, 1)
            batch(0, 0, 1)
            batch(1, 1, 2)
            with act.Fori(1, turns - 1) as i:
                batch(i * 2, 0, i * 2 + 1)
                batch(i * 2 + 1, 1, i * 2 + 2)
            batch(NB - 2, 0, NB - 1, False)
            batch(NB - 1, 1, NB, False)
            act.wait_ge(s["sums"], NB)
            act.activation(inv[:], squares, ACT.Sqrt).then_inc(s["inv"], 1)

        @block.tensor
        def _(pe):
            pe.wait_ge(s["scaled"], 1)

            def turn(par, count):
                pe.wait_ge(s["xn"], count)
                wait(pe, s["xnt"], count - 2)
                for t in range(NT):
                    ins = pe.transpose(banks[par][:, t * P:(t + 1) * P], xn[:, par, t, :], K.ident[:])
                ins.then_inc(s["turned"], 1)

            def batch(par, count, more=True):
                if more:
                    turn(1 - par, count + 1)
                pe.wait_ge(s["xnt"], count)
                wait(pe, s["q_read"], count - 2)
                pe.matmul(banks[2 + par][:, 0:S], W["q"], xnt[:, par, :], start=True, stop=True).then_inc(s["q_full"], 1)

            def head_sums(par, count):
                wait(pe, s["sums"], count - 2)
                pe.wait_ge(s["squared"], count)
                for t in range(NT):
                    tokens = slice(t * P, (t + 1) * P)
                    pe.matmul(banks[4 + par][:, 2 * t * H:(2 * t + 1) * H], q[:, par, tokens], guide_block[:], start=True, stop=True)
                    ins = pe.matmul(banks[4 + par][:, (2 * t + 1) * H:(2 * t + 2) * H], square[:, par, tokens], own_block[:],
                                    start=True, stop=True)
                ins.then_inc(s["summed"], 1)
            turn(0, 1)
            batch(0, 1)
            batch(1, 2)
            pe.wait_ge(s["blocks"], 1)
            head_sums(0, 1)
            with pe.Fori(1, turns - 1) as i:
                batch(0, i * 2 + 1)
                head_sums(1, i * 2)
                batch(1, i * 2 + 2)
                head_sums(0, i * 2 + 1)
            batch(0, NB - 1)
            head_sums(1, NB - 2)
            batch(1, NB, False)
            head_sums(0, NB - 1)
            head_sums(1, NB)
            pe.wait_ge(s["ends"], 2)
            pe.transpose(banks[4][0:2, 0:P], ends[:], K.ident[:]).then_inc(s["mm"], 1)
            pe.wait_ge(s["spread"], 1)
            pe.matmul(banks[5][:, 0:2], ones[:], diag[:], start=True, stop=True).then_inc(s["all"], 1)

        @block.gpsimd
        def _(pool):
            own = Chain(pool, s["pool_own"])
            own.done(pool.memset(g_half[:], -0.5))
            own.done(pool.memset(ones[:], 1.0))
            own.done(pool.tensor_tensor(g_sq[:], K.guide[:], K.guide[:], ALU.mult))
            pool.wait_ge(s["guided"], 1)
            own.done(pool.tensor_tensor(g_inv[:], g_sum[:], g_half[:], ALU.pow))
            own.done(pool.tensor_tensor(guide[:].rearrange("p (h d) -> p h d", d=D8),
                                        K.guide[:].rearrange("p (h d) -> p h d", d=D8),
                                        g_inv[:].unsqueeze(2).to_broadcast([P, H, D8]), ALU.mult))


            def but_registers(dst, src, fill):
                return pool.affine_select(out=dst.rearrange("p (b t) -> p b t", t=NT), in_=src.rearrange("p (b t) -> p b t", t=NT),
                                          compare_op=ALU.is_ge, fill=fill, base=-REG, pattern=[[0, NB], [P, NT]],
                                          channel_multiplier=1)
            pool.wait_ge(s["inv"], 2)
            but_registers(low[:], sim[:], BIG)
            but_registers(top[:], sim[:], -BIG).then_inc(s["pos"], 1)
            pool.wait_ge(s["pos"], 2)
            but_registers(first_q[:], first[:], 1.0)
            but_registers(first_k[:], first[:], 0.0)
            but_registers(second_k[:], second[:], 0.0).then_inc(s["pos"], 1)

        @block.vector
        def _(dve):
            stat_dve(dve)
            if "scale" in W:
                dve.wait_ge(s["norm_ready"], 1)
                dve.tensor_scalar(W["scale"][0], W["scale"][0], W["scale"][1], None, ALU.mult).then_inc(s["scaled"], 1)
            else:
                dve.memset(sim[:], 0.0).then_inc(s["scaled"], 1)
            dve.wait_ge(s["pool_own"], 3)
            dve.tensor_reduce(g_sum[:], g_sq[:].rearrange("p (h d) -> p h d", d=D8), AX.X, ALU.add).then_inc(s["guided"], 1)

            own = Chain(dve, s["own"])
            own.done(dve.tensor_copy(own_block[:], K.own_head[:].rearrange("p (h q) -> p h q", q=REG)[:, :, 0]))
            dve.wait_ge(s["pool_own"], 5)
            own.done(dve.tensor_tensor(g_sq[:], guide[:], K.ident[:], ALU.mult))
            own.done(dve.tensor_reduce(g_column[:], g_sq[:], AX.X, ALU.add))
            dve.tensor_scalar(guide_block[:], own_block[:], g_column[:], None, ALU.mult).then_inc(s["blocks"], 1)

            def squares_of(par, count):
                dve.wait_ge(s["q_read"], count)
                wait(dve, s["summed"], count - 2)
                dve.tensor_tensor(square[:, par, :], q[:, par, :], q[:, par, :], ALU.mult).then_inc(s["squared"], 1)

            def keep(n, par, count):
                dve.wait_ge(s["summed"], count)
                dve.tensor_copy(dots_squares[:, bass.ds(n * NT, NT)],
                                banks[4 + par][:, 0:NT * 2 * H].rearrange("p (t z h) -> p t z h", t=NT, z=2)).then_inc(s["sums"], 1)
            squares_of(0, 1)
            squares_of(1, 2)
            keep(0, 0, 1)
            with dve.Fori(1, turns) as i:
                squares_of(0, i * 2 + 1)
                keep(i * 2 - 1, 1, i * 2)
                squares_of(1, i * 2 + 2)
                keep(i * 2, 0, i * 2 + 1)
            keep(NB - 1, 1, NB)
            dve.wait_ge(s["inv"], 1)
            dve.wait_ge(s["sums"], NB)
            own.done(dve.reciprocal(inv[:], inv[:]))
            own.done(dve.tensor_tensor(dots, dots, inv[:], ALU.mult))
            own.done(dve.tensor_reduce(sim[:], dots, AX.X, ALU.add))
            dve.tensor_scalar(sim[:], sim[:], 1.0 / H, None, ALU.mult).then_inc(s["inv"], 1)
            dve.wait_ge(s["pos"], 1)
            dve.tensor_reduce(ends[:, 0:1], low[:], AX.X, ALU.min, negate=True).then_inc(s["ends"], 1)
            dve.tensor_reduce(ends[:, 1:2], top[:], AX.X, ALU.max).then_inc(s["ends"], 1)
            dve.wait_ge(s["mm"], 1)
            own.done(dve.tensor_reduce(two[:], banks[4][0:2, 0:P], AX.X, ALU.max))
            dve.tensor_scalar(diag[:], K.ident[0:2, 0:2], two[:], None, ALU.mult).then_inc(s["spread"], 1)
            dve.wait_ge(s["all"], 1)
            own.done(dve.tensor_copy(both[:], banks[5][:, 0:2]))
            own.done(dve.tensor_tensor(span[:], both[:, 0:1], both[:, 1:2], ALU.add))
            own.done(dve.reciprocal(span[:], span[:]))
            own.done(dve.tensor_scalar(sim[:], sim[:], both[:, 0:1], span[:], ALU.add, ALU.mult))
            own.done(dve.tensor_scalar(first[:], sim[:], 0.9, None, ALU.is_gt))
            dve.tensor_scalar(second[:], first[:], -1.0, 1.0, ALU.mult, ALU.add).then_inc(s["pos"], 1)
            dve.wait_ge(s["pos"], 3)
            own.done(dve.tensor_scalar(K.mask_q[:, :, 0], first_q[:], -BIG, None, ALU.mult))
            own.done(dve.tensor_scalar(K.mask_q[:, :, 1], first_q[:], BIG, -BIG, ALU.mult, ALU.add))
            own.done(dve.tensor_copy(K.mask_k[:, :, 0], second_k[:]))
            own.done(dve.tensor_copy(K.mask_k[:, :, 1], first_k[:]))



E8 = 8
CAP = 2 * S // E8
HID = 512
HC = HID // P


def route(nc, K, name, W):
    with ExitStack() as ctx:
        ctx.enter_context(nc.cleanup_on_exit())
        def sb(n, shape, dt=F32):
            return ctx.enter_context(nc.sbuf_tensor(f"{name}_r_{n}", shape, dt))

        s = {n: nc.alloc_semaphore(name=f"{name}_r_{n}") for n in (
            "stat_dve", "var_ready", "rstd_ready", "norm_ready", "xn", "turned", "xnt", "logits", "copied",
            "less_max", "exps", "probs", "by_expert", "own", "slots", "by_token")}
        xn, xnt = sb("xn", [P, 2, NT, C]), sb("xnt", [P, 2, S])
        logit = sb("logit", [P, NT, NB, E8])
        greatest, total, inv = sb("greatest", [P, NT * NB]), sb("total", [P, NT * NB]), sb("inv", [P, NT * NB])
        work = [sb("work0", [P, S]), sb("work1", [P, S])]
        top, taken, place = sb("top", [P, 8]), sb("taken", [P, S]), sb("place", [P, S])
        zeros = sb("zeros", [P, S])
        stat_dve, stat_act = norm_stats(K, s)
        block = ctx.enter_context(nc.Block(name + "_r"))
        banks = K.banks
        turns = NB // 2

        @block.scalar
        def _(act):
            stat_act(act)
            act.wait_ge(s["norm_ready"], 1)

            def normed(n, par):
                for t in range(NT):
                    tile = bass.ds(n * NT + t, 1)
                    ins = act.activation(xn[:, par, t, :], K.X[:, tile, :].rearrange("p a c -> p (a c)"), ACT.Identity,
                                         bias=K.shift[:, tile], scale=K.rstd[:, tile])
                ins.then_inc(s["xn"], 1)

            def batch(n, par, count, more=True):
                act.wait_ge(s["turned"], count)
                act.activation(xnt[:, par, :], banks[par][:, 0:S], ACT.Copy).then_inc(s["xnt"], 1)
                if more:
                    normed(n + 2, par)
            normed(0, 0)
            normed(1, 1)
            with act.Fori(0, turns - 1) as i:
                batch(i * 2, 0, i * 2 + 1)
                batch(i * 2 + 1, 1, i * 2 + 2)
            batch(NB - 2, 0, NB - 1, False)
            batch(NB - 1, 1, NB, False)
            act.wait_ge(s["less_max"], 1)
            act.activation(K.prob[:], logit[:], ACT.Exp).then_inc(s["exps"], 1)

        @block.tensor
        def _(pe):
            def turn(par, count):
                pe.wait_ge(s["xn"], count)
                wait(pe, s["xnt"], count - 2)
                for t in range(NT):
                    ins = pe.transpose(banks[par][:, t * P:(t + 1) * P], xn[:, par, t, :], K.ident[:])
                ins.then_inc(s["turned"], 1)

            def batch(par, count, more=True):
                if more:
                    turn(1 - par, count + 1)
                pe.wait_ge(s["xnt"], count)
                wait(pe, s["copied"], count - 2)
                for t in range(NT):
                    ins = pe.matmul(banks[2 + par][:, t * E8:(t + 1) * E8], xnt[:, par, t * P:(t + 1) * P], W["gate"],
                                    start=True, stop=True)
                ins.then_inc(s["logits"], 1)
            turn(0, 1)
            batch(0, 1)
            batch(1, 2)
            with pe.Fori(1, turns - 1) as i:
                batch(0, i * 2 + 1)
                batch(1, i * 2 + 2)
            batch(0, NB - 1)
            batch(1, NB, False)
            pe.wait_ge(s["probs"], 1)
            for t in range(NT):
                ins = pe.transpose(banks[4][:, t * P:(t + 1) * P], K.prob[:, t].rearrange("p b e -> p (b e)"), K.ident[:])
            ins.then_inc(s["by_expert"], 1)
            pe.wait_ge(s["slots"], 1)
            for t in range(NT):
                ins = pe.transpose(banks[5][:, t * P:(t + 1) * P], place[:, t * P:(t + 1) * P], K.ident[:])
            ins.then_inc(s["by_token"], 1)

        @block.vector
        def _(dve):
            stat_dve(dve)

            def batch(n, par, count):
                dve.wait_ge(s["logits"], count)
                dve.tensor_copy(logit[:, :, bass.ds(n, 1), :], banks[2 + par][:, 0:NT * E8].rearrange(
                    "p (t a e) -> p t a e", a=1, e=E8)).then_inc(s["copied"], 1)
            batch(0, 0, 1)
            batch(1, 1, 2)
            with dve.Fori(1, turns) as i:
                batch(i * 2, 0, i * 2 + 1)
                batch(i * 2 + 1, 1, i * 2 + 2)
            own = Chain(dve, s["own"])
            by_token = logit[:].rearrange("p t b e -> p (t b) e")
            prob = K.prob[:].rearrange("p t b e -> p (t b) e")
            dve.wait_ge(s["copied"], NB)
            own.done(dve.tensor_reduce(greatest[:], by_token, AX.X, ALU.max))
            dve.tensor_tensor(by_token, by_token, greatest[:].unsqueeze(2).to_broadcast([P, NT * NB, E8]),
                              ALU.subtract).then_inc(s["less_max"], 1)
            dve.wait_ge(s["exps"], 1)
            own.done(dve.tensor_reduce(total[:], prob, AX.X, ALU.add))
            own.done(dve.reciprocal(inv[:], total[:]))
            own.done(dve.memset(zeros[:], 0.0))
            dve.tensor_tensor(prob, prob, inv[:].unsqueeze(2).to_broadcast([P, NT * NB, E8]), ALU.mult).then_inc(s["probs"], 1)
            dve.wait_ge(s["by_expert"], 1)
            own.done(dve.tensor_copy(work[0][:], banks[4][:, 0:S]))
            for r in range(CAP // 8):
                own.done(dve.max(top[:], work[r % 2][:]))
                own.done(dve.match_replace(work[(r + 1) % 2][:], top[:], work[r % 2][:], -1.0))
            own.done(dve.tensor_scalar(taken[:], work[0][:], 0.0, None, ALU.is_lt))
            own.done(dve.tensor_tensor_scan(place[:], taken[:], zeros[:], 0.0, ALU.add, ALU.add))
            own.done(dve.tensor_tensor(place[:], place[:], taken[:], ALU.mult))
            dve.tensor_scalar(place[:], place[:], -1.0, None, ALU.add).then_inc(s["slots"], 1)
            dve.wait_ge(s["by_token"], 1)
            own.done(dve.tensor_copy(K.slot[:].rearrange("p t b e -> p t (b e)"),
                                     banks[5][:, 0:S].rearrange("p (t j) -> p t j", t=NT)))


EXPERT_BANK = {"gather": (0, 1), "turn": (0, 1, 0, 1)}


def expert_schedule(do_a, do_b, do_e):
    a = {0: [("norm", 0), ("onehot", 0)], 2: [("gather", 0), ("gather", 1)], 4: [("turn", 0)], 5: [("turn", 1)],
         6: [("turn", 2)], 7: [("turn", 3)]}
    e = {1: [("scatter", 0)], 2: [("add", 0)]}
    pieces = []
    for slot in range(E8 + 1):
        if do_b and slot < E8:
            pieces.append(("up", slot))
        if do_e:
            pieces += e.get(slot, [])
        if do_a:
            pieces += a.get(slot, [])
        if do_b and slot > 0:
            pieces.append(("down", slot - 1))
            if slot % 4 == 0:
                pieces.append(("kept", slot // 4 - 1))
    return pieces


def experts(nc, K, name, W):
    U = 2
    UNITS = NB // U
    with ExitStack() as outer:
        outer.enter_context(nc.cleanup_on_exit())
        K.prob = outer.enter_context(nc.sbuf_tensor(f"{name}_prob", [P, NT, NB, E8], F32))
        K.slot = outer.enter_context(nc.sbuf_tensor(f"{name}_slot", [P, NT, NB, E8], F32))
        route(nc, K, name, W)
        ctx = outer

        def sb(n, shape, dt=F32):
            return ctx.enter_context(nc.sbuf_tensor(f"{name}_{n}", shape, dt))

        s = {n: nc.alloc_semaphore(name=f"{name}_{n}") for n in (
            "xn", "onehot", "weighed", "full0", "full1", "drained0", "drained1", "up", "gelu", "down", "kept",
            "scattered", "added", "stats", "counted", "waited")}
        full, drained = [s["full0"], s["full1"]], [s["drained0"], s["drained1"]]
        fills = [3, 3]
        xn = sb("xn", [P, 2, U, NT, C])
        g = sb("g", [P, 2, NT, E8, U, CAP])
        gp = sb("gp", [P, 2, NT, E8, U, CAP])
        gpt = sb("gpt", [P, 2, NT, E8, P])
        xi = sb("xi", [P, 2, E8, U, CAP])
        ht = sb("ht", [P, 2, HC, P])
        ys = sb("ys", [P, 2, E8, C])
        count_i, count = sb("count_i", [P, CAP], I32), sb("count", [P, CAP])
        Hb, Yb, Rb, Mb = K.Sb, K.Tb, K.Ob, K.Mb
        block = ctx.enter_context(nc.Block(name))

        def fill_tallies():
            return [Tally(s["full0"], fills[0]), Tally(s["full1"], fills[1])]

        def bank_of(tallies, what, i):
            if what not in EXPERT_BANK:
                return None, None
            b = EXPERT_BANK[what][i]
            return b, tallies[b].add()

        @block.tensor
        def _(pe):
            fill = fill_tallies()
            xn_t, onehot_t, weighed_t = Tally(s["xn"], 1), Tally(s["onehot"], 4), Tally(s["weighed"], 4)
            up_t, gelu_t, kept_t, down_t = Tally(s["up"], E8), Tally(s["gelu"], E8), Tally(s["kept"], 2), Tally(s["down"], 2)
            tallies = fill + [xn_t, onehot_t, weighed_t, up_t, gelu_t, kept_t, down_t]

            def step(n, par, do_a, do_b, do_e):
                nxt = 1 - par
                for what, i in expert_schedule(do_a, do_b, do_e):
                    b, filling = bank_of(fill, what, i)
                    if b is not None:
                        bank = Mb[b]
                        wait(pe, drained[b], fill[b].value(1))
                    if what == "gather":
                        if i == 0:
                            pe.wait_ge(s["xn"], xn_t.add())
                        pe.wait_ge(s["onehot"], onehot_t.add(NT))
                        for t in range(NT):
                            ins = pe.matmul(bank[:], xn[:, nxt, i, t, :], g[:, nxt, t, :, i, :], start=(t == 0),
                                            stop=(t == NT - 1))
                        ins.then_inc(full[b], 1)
                    elif what == "turn":
                        if i == 0:
                            pe.wait_ge(s["weighed"], weighed_t.add(4))
                        for j in range(4):
                            ins = pe.transpose(bank[:, j * P:(j + 1) * P],
                                               gp[:, nxt, i // 2, 4 * (i % 2) + j].rearrange("p u l -> p (u l)"), K.ident[:])
                        ins.then_inc(full[b], 1)
                    elif what == "up":
                        if i == 0:
                            for z in range(2):
                                pe.wait_ge(drained[z], fill[z].value())
                        wait(pe, s["gelu"], up_t.add() - 2)
                        for c in range(HC):
                            ins = pe.matmul(Hb[i % 2][:, c * P:(c + 1) * P], W["w1"][:, i, c * P:(c + 1) * P],
                                            xi[:, par, i].rearrange("p u l -> p (u l)"), start=True, stop=True)
                        ins.then_inc(s["up"], 1)
                    elif what == "down":
                        if i % 4 == 0:
                            wait(pe, s["kept"], down_t.add() - 2)
                        pe.wait_ge(s["gelu"], gelu_t.add())
                        for c in range(HC):
                            ins = pe.matmul(Yb[i // 4][:, (i % 4) * C:(i % 4 + 1) * C], ht[:, i % 2, c, :],
                                            W["w2"][:, i, c, :], start=(c == 0), stop=(c == HC - 1))
                        ins.then_inc(s["down"], 1)
                    elif what == "scatter":
                        pe.wait_ge(s["kept"], kept_t.add(2))
                        for u in range(U):
                            rows = slice(u * CAP, (u + 1) * CAP)
                            for t in range(NT):
                                for e in range(E8):
                                    at = Rb[u][:, t * C:(t + 1) * C]
                                    ins = pe.matmul(at, gpt[rows, nxt, t, e, :], ys[rows, nxt, e, :], start=(e == 0),
                                                    stop=(e == E8 - 1))
                        ins.then_inc(s["scattered"], 1)

            batches(pe, tallies, step, UNITS)

        @block.scalar
        def _(act):
            fill = fill_tallies()
            up_t, down_t = Tally(s["up"], E8), Tally(s["down"], E8)
            tallies = fill + [up_t, down_t]

            def step(n, par, do_a, do_b, do_e):
                nxt = 1 - par
                for what, i in expert_schedule(do_a, do_b, do_e):
                    b, filling = bank_of(fill, what, i)
                    if what == "norm":
                        for k in range(U * NT):
                            tile = bass.ds((n + 1) * U * NT + k, 1)
                            ins = act.activation(xn[:, nxt, k // NT, k % NT, :], K.X[:, tile, :].rearrange("p a c -> p (a c)"),
                                                 ACT.Identity, bias=K.shift[:, tile], scale=K.rstd[:, tile])
                        ins.then_inc(s["xn"], 1)
                    elif what == "gather":
                        act.wait_ge(full[b], filling)
                        act.activation(xi[:, nxt, :, i, :], Mb[b][:].rearrange("p (e l) -> p e l", l=CAP),
                                       ACT.Copy).then_inc(drained[b], 1)
                    elif what == "up":
                        act.wait_ge(s["up"], up_t.add())
                        wait(act, s["down"], down_t.add() - 2)
                        act.activation(ht[:, i % 2].rearrange("p c l -> p (c l)"), Hb[i % 2][:], ACT.Gelu).then_inc(s["gelu"], 1)

            batches(act, tallies, step, UNITS)

        @block.vector
        def _(dve):
            fill = fill_tallies()
            down_t, scattered_t, added_t, stats_t = Tally(s["down"], E8), Tally(s["scattered"], 1), Tally(s["added"], U), Tally(s["stats"], 4)
            tallies = fill + [down_t, scattered_t, added_t, stats_t]

            def step(n, par, do_a, do_b, do_e):
                nxt = 1 - par
                for what, i in expert_schedule(do_a, do_b, do_e):
                    b, filling = bank_of(fill, what, i)
                    if what == "onehot":
                        for u in range(U):
                            for t in range(NT):
                                slot = K.slot[:, t, bass.ds((n + 1) * U + u, 1), :].rearrange("p a e -> p (a e)")
                                dve.tensor_tensor(g[:, nxt, t, :, u, :], count[:].unsqueeze(1).to_broadcast([P, E8, CAP]),
                                                  slot.unsqueeze(2).to_broadcast([P, E8, CAP]),
                                                  ALU.is_equal).then_inc(s["onehot"], 1)
                    elif what == "turn":
                        dve.wait_ge(full[b], filling)
                        dve.tensor_copy(gpt[:, nxt, i // 2, 4 * (i % 2):4 * (i % 2) + 4, :],
                                        Mb[b][:].rearrange("p (e j) -> p e j", j=P)).then_inc(drained[b], 1)
                    elif what == "kept":
                        dve.wait_ge(s["down"], down_t.add(4))
                        dve.tensor_copy(ys[:, par, 4 * i:4 * i + 4, :],
                                        Yb[i][:].rearrange("p (e c) -> p e c", c=C)).then_inc(s["kept"], 1)
                    elif what == "add":
                        dve.wait_ge(s["scattered"], scattered_t.add())
                        for u in range(U):
                            x = K.X[:, bass.ds(((n - 1) * U + u) * NT, NT), :]
                            dve.tensor_tensor(x, x, Rb[u][:, 0:NT * C].rearrange("p (t c) -> p t c", c=C),
                                              ALU.add).then_inc(s["added"], 1)
                        dve.wait_ge(s["added"], added_t.add(U))
                        for k in range(U * NT):
                            tile = bass.ds((n - 1) * U * NT + k, 1)
                            dve.bn_stats(K.moments[:, tile, :].rearrange("p a m -> p (a m)"),
                                         K.X[:, tile, :].rearrange("p a c -> p (a c)")).then_inc(s["stats"], 1)
                        stats_t.add(4)

            dve.wait_ge(s["counted"], 2)
            batches(dve, tallies, step, UNITS)
            dve.wait_ge(s["stats"], stats_t.value())

        @block.gpsimd
        def _(pool):
            onehot_t = Tally(s["onehot"], 4)
            pool.iota(count_i[:], pattern=[[1, CAP]], base=0, channel_multiplier=0).then_inc(s["counted"], 1)
            pool.wait_ge(s["counted"], 1)
            pool.tensor_copy(count[:], count_i[:]).then_inc(s["counted"], 1)

            def step(n, par, do_a, do_b, do_e):
                nxt = 1 - par
                for what, i in expert_schedule(do_a, do_b, do_e):
                    if what == "onehot":
                        for u in range(U):
                            for t in range(NT):
                                pool.wait_ge(s["onehot"], onehot_t.add())
                                prob = K.prob[:, t, bass.ds((n + 1) * U + u, 1), :].rearrange("p a e -> p (a e)")
                                pool.tensor_tensor(gp[:, nxt, t, :, u, :], g[:, nxt, t, :, u, :],
                                                   prob.unsqueeze(2).to_broadcast([P, E8, CAP]), ALU.mult).then_inc(s["weighed"], 1)

            batches(pool, [onehot_t], step, UNITS)



def recurrent(nc, K, name, W):
    with ExitStack() as ctx:
        ctx.enter_context(nc.cleanup_on_exit())
        def sb(n, shape, dt=F32):
            return ctx.enter_context(nc.sbuf_tensor(f"{name}_{n}", shape, dt))

        s = {n: nc.alloc_semaphore(name=f"{name}_{n}") for n in (
            "stat_dve", "var_ready", "rstd_ready", "norm_ready", "wt_full", "wt", "lam", "rate_own", "rate",
            "xn", "turned", "xnt", "gates", "gated", "inputs", "decay", "root", "own", "states", "back", "added", "stats")}
        xn, xnt = sb("xn", [P, 2, NT, C]), sb("xnt", [P, 2, S])
        r, i_gate = sb("r", [P, NB, S]), sb("i_gate", [P, 2, S])
        ix, a, root = sb("ix", [P, NB, S]), sb("a", [P, NB, S]), sb("root", [P, NB, S])
        b, y = sb("b", [P, 2, S]), sb("y", [P, 2, S])
        wt = sb("wt", [P, 2, C])
        lam, soft, rate = sb("lam", [P, 3]), sb("soft", [P, 2]), sb("rate", [P, 1])
        stat_dve, stat_act = norm_stats(K, s)
        block = ctx.enter_context(nc.Block(name))
        banks = K.banks
        turns = NB // 2

        @block.scalar
        def _(act):
            act.wait_ge(s["lam"], 1)
            act.activation(soft[:, 0:1], lam[:, 0:1], ACT.Exp, scale=-1.0).then_inc(s["rate_own"], 1)
            act.wait_ge(s["rate_own"], 1)
            act.activation(soft[:, 1:2], soft[:, 0:1], ACT.Ln, bias=1.0).then_inc(s["rate_own"], 1)
            act.wait_ge(s["wt_full"], 1)
            act.activation(wt[:].rearrange("p w c -> p (w c)"), banks[0][:, 0:2 * C], ACT.Copy).then_inc(s["wt"], 1)
            stat_act(act)
            act.wait_ge(s["norm_ready"], 1)

            def normed(n, par):
                for t in range(NT):
                    tile = bass.ds(n * NT + t, 1)
                    ins = act.activation(xn[:, par, t, :], K.X[:, tile, :].rearrange("p a c -> p (a c)"), ACT.Identity,
                                         bias=K.shift[:, tile], scale=K.rstd[:, tile])
                ins.then_inc(s["xn"], 1)

            def batch(n, par, count, more=True):
                act.wait_ge(s["turned"], count)
                wait(act, s["inputs"], count - 2)
                act.activation(xnt[:, par, :], banks[par][:, 0:S], ACT.Copy).then_inc(s["xnt"], 1)
                if more:
                    normed(n + 2, par)
                act.wait_ge(s["gates"], count)
                act.activation(r[:, bass.ds(n, 1), :].rearrange("p a s -> p (a s)"), banks[2 + par][:, 0:S], ACT.Sigmoid, bias=W["ba"])
                act.activation(i_gate[:, par, :], banks[2 + par][:, S:2 * S], ACT.Sigmoid, bias=W["bx"]).then_inc(s["gated"], 1)
            normed(0, 0)
            normed(1, 1)
            batch(0, 0, 1)
            batch(1, 1, 2)
            with act.Fori(1, turns - 1) as i:
                batch(i * 2, 0, i * 2 + 1)
                batch(i * 2 + 1, 1, i * 2 + 2)
            batch(NB - 2, 0, NB - 1, False)
            batch(NB - 1, 1, NB, False)
            act.wait_ge(s["rate"], 1)
            act.wait_ge(s["gated"], NB)
            act.activation(a[:], r[:], ACT.Exp, scale=rate[:]).then_inc(s["decay"], 1)
            act.wait_ge(s["decay"], 1)
            act.activation(root[:], a[:], ACT.Square).then_inc(s["decay"], 1)
            act.wait_ge(s["decay"], 2)
            act.activation(root[:], root[:], ACT.Sqrt, scale=-1.0, bias=1.0).then_inc(s["root"], 1)

        @block.tensor
        def _(pe):
            pe.transpose(banks[0][:, 0:C], W["wa"], K.ident[:])
            pe.transpose(banks[0][:, C:2 * C], W["wx"], K.ident[:]).then_inc(s["wt_full"], 1)
            pe.wait_ge(s["wt"], 1)

            def turn(par, count):
                pe.wait_ge(s["xn"], count)
                wait(pe, s["xnt"], count - 2)
                for t in range(NT):
                    ins = pe.transpose(banks[par][:, t * P:(t + 1) * P], xn[:, par, t, :], K.ident[:])
                ins.then_inc(s["turned"], 1)

            def batch(par, count, more=True):
                if more:
                    turn(1 - par, count + 1)
                pe.wait_ge(s["xnt"], count)
                wait(pe, s["gated"], count - 2)
                for w in range(2):
                    ins = pe.matmul(banks[2 + par][:, w * S:(w + 1) * S], wt[:, w, :], xnt[:, par, :], start=True, stop=True)
                ins.then_inc(s["gates"], 1)
            turn(0, 1)
            batch(0, 1)
            batch(1, 2)
            with pe.Fori(1, turns - 1) as i:
                batch(0, i * 2 + 1)
                batch(1, i * 2 + 2)
            batch(0, NB - 1)
            batch(1, NB, False)

            def back(par, count):
                pe.wait_ge(s["states"], count)
                for t in range(NT):
                    ins = pe.transpose(banks[4 + par][:, t * P:(t + 1) * P], y[:, par, t * P:(t + 1) * P], K.ident[:])
                ins.then_inc(s["back"], 1)
            with pe.Fori(0, turns) as i:
                back(0, i * 2 + 1)
                back(1, i * 2 + 2)

        @block.vector
        def _(dve):
            dve.tensor_scalar(lam[:, 2:3], W["lam"], -1.0, None, ALU.mult).then_inc(s["own"], 1)
            dve.wait_ge(s["own"], 1)
            dve.tensor_scalar(lam[:, 1:2], lam[:, 2:3], 0.0, None, ALU.max).then_inc(s["own"], 1)
            dve.tensor_tensor(lam[:, 0:1], W["lam"], lam[:, 2:3], ALU.max).then_inc(s["lam"], 1)
            stat_dve(dve)
            dve.wait_ge(s["rate_own"], 2)
            dve.wait_ge(s["own"], 2)
            dve.tensor_tensor(rate[:], lam[:, 1:2], soft[:, 1:2], ALU.add).then_inc(s["own"], 1)
            dve.wait_ge(s["own"], 3)
            dve.tensor_scalar(rate[:], rate[:], -8.0, None, ALU.mult).then_inc(s["rate"], 1)

            def batch(n, par, count):
                dve.wait_ge(s["gated"], count)
                dve.tensor_tensor(ix[:, bass.ds(n, 1), :].rearrange("p a s -> p (a s)"), i_gate[:, par, :], xnt[:, par, :],
                                  ALU.mult).then_inc(s["inputs"], 1)
            with dve.Fori(0, turns) as i:
                batch(i * 2, 0, i * 2 + 1)
                batch(i * 2 + 1, 1, i * 2 + 2)
            dve.wait_ge(s["inputs"], NB)
            dve.wait_ge(s["root"], 1)
            own = 3

            def scan(n, par, count):
                one = bass.ds(n, 1)
                dve.tensor_tensor(b[:, par, :], root[:, one, :].rearrange("p a s -> p (a s)"),
                                  ix[:, one, :].rearrange("p a s -> p (a s)"), ALU.mult).then_inc(s["own"], 1)
                dve.wait_ge(s["own"], count + own)
                dve.tensor_tensor_scan(y[:, par, :], a[:, one, :].rearrange("p a s -> p (a s)"), b[:, par, :], 0.0,
                                       ALU.mult, ALU.add).then_inc(s["states"], 1)

            def add(n, par, count):
                dve.wait_ge(s["back"], count)
                x = K.X[:, bass.ds(n * NT, NT), :]
                dve.tensor_tensor(x, x, banks[4 + par][:, 0:S].rearrange("p (t c) -> p t c", c=C), ALU.add).then_inc(s["added"], 1)
                dve.wait_ge(s["added"], count)
                for t in range(NT):
                    tile = bass.ds(n * NT + t, 1)
                    dve.bn_stats(K.moments[:, tile, :].rearrange("p a m -> p (a m)"),
                                 K.X[:, tile, :].rearrange("p a c -> p (a c)")).then_inc(s["stats"], 1)
            with dve.Fori(0, turns) as i:
                scan(i * 2, 0, i * 2 + 1)
                scan(i * 2 + 1, 1, i * 2 + 2)
                add(i * 2, 0, i * 2 + 1)
                add(i * 2 + 1, 1, i * 2 + 2)
            dve.wait_ge(s["stats"], TILES)



D64 = 64
PAIRS = H // 2
WIDE_BANK = {"norm": (0,), "qk": (1, 0, 0, 1, 1, 0, 0, 1), "attn": (1, 0, 1, 0), "v": (1, 0, 0, 1), "project": (1,),
             "turnmax": (0,)}


def wide_schedule(do_a, do_b, do_e):
    a = {0: [("norm", 0)], 12: [("split", 0)], 14: [("turnmax", 0)]}
    e = {}
    for n in range(4):
        a[1 + n] = [("qk", 2 * n), ("qk", 2 * n + 1)]
        a[5 + n] = [("v", n)]
        e[1 + n] = [("attn", n)]
    for n in range(PAIRS):
        a[4 + n] = a.get(4 + n, []) + [("max", 2 * n), ("max", 2 * n + 1)]
    e[6] = [("project", 0)]
    pieces = []
    for slot in range(H + 1):
        if do_b and slot < H:
            pieces.append(("score", slot))
        if do_a:
            pieces += a.get(slot, [])
        if do_e:
            pieces += e.get(slot, [])
        if do_b and slot > 0:
            pieces.append(("value", slot - 1))
            if slot % 2 == 0:
                pieces.append(("divide", slot // 2 - 1))
    return pieces


def wide_attention(nc, K, name, W):
    fills = [sum(b == m for banks in WIDE_BANK.values() for b in banks) for m in range(2)]
    with ExitStack() as ctx:
        ctx.enter_context(nc.cleanup_on_exit())
        def sb(n, shape, dt=F32):
            return ctx.enter_context(nc.sbuf_tensor(f"{name}_{n}", shape, dt))

        s = {n: nc.alloc_semaphore(name=f"{name}_{n}") for n in (
            "stat_dve", "var_ready", "rstd_ready", "norm_ready", "pool_set", "dve_set", "xn", "full0", "full1",
            "drained0", "drained1", "half", "waited", "pool_own", "scores", "maxed", "dve_own", "shifted", "scored",
            "exps", "valued", "divided", "biased", "stats")}
        full, drained = [s["full0"], s["full1"]], [s["drained0"], s["drained1"]]
        xn, xnt = sb("xn", [P, 2, NT, C]), sb("xnt", [P, 2, S])
        qk = sb("qk", [P, 2, PAIRS, 2, S])
        qk16 = sb("qk16", [P, 2, PAIRS, 2, S], BF16)
        va = sb("va", [P, 2, NT, H, D64 + 1])
        mx, mrest = sb("mx", [P, 2, NT, H]), sb("mrest", [P, NT, H])
        parts = sb("parts", [P, 2, NT, 2, 64], BF16)
        shift = sb("shift", [P, 2, S], BF16)
        pick = sb("pick", [P, H, P], BF16)
        pr = sb("pr", [P, 2, 2 * S])
        rc = sb("rc", [P, 4])
        att = sb("att", [P, 2, NT, H, D64])
        att_t = sb("att_t", [P, PAIRS, S])
        Sb, Tb, Ob, Mb = K.Sb, K.Tb, K.Ob, K.Mb
        stat_dve, stat_act = norm_stats(K, s)
        block = ctx.enter_context(nc.Block(name))
        POOL_SETS = 6

        def rows(h):
            return slice(64 * (h % 2), 64 * (h % 2) + 64)

        def fill_tallies():
            return [Tally(s["full0"], fills[0]), Tally(s["full1"], fills[1])]

        def bank_of(tallies, what, i):
            if what not in WIDE_BANK:
                return None, None
            b = WIDE_BANK[what][i]
            return b, tallies[b].add()

        @block.tensor
        def _(pe):
            fill = fill_tallies()
            xn_t, half_t, maxed_t = Tally(s["xn"], 1), Tally(s["half"], PAIRS), Tally(s["maxed"], H)
            shifted_t, exps_t, scored_t = Tally(s["shifted"], 1), Tally(s["exps"], H), Tally(s["scored"], H)
            o_t, divided_t = Tally(s["divided"], PAIRS), Tally(s["divided"], PAIRS)
            tallies = fill + [xn_t, half_t, maxed_t, shifted_t, exps_t, scored_t, o_t, divided_t]

            def step(n, par, do_a, do_b, do_e):
                nxt = 1 - par
                for what, i in wide_schedule(do_a, do_b, do_e):
                    b, filling = bank_of(fill, what, i)
                    if b is not None:
                        bank = Mb[b]
                        wait(pe, drained[b], fill[b].value(1))
                    if what == "norm":
                        pe.wait_ge(s["xn"], xn_t.add())
                        for t in range(NT):
                            ins = pe.transpose(bank[:, t * P:(t + 1) * P], xn[:, nxt, t, :], K.ident[:])
                        ins.then_inc(full[b], 1)
                    elif what == "qk":
                        if i == 0:
                            wait(pe, drained[0], fill[0].value())
                        for z, w in enumerate((W["wq"], W["wk"])):
                            ins = pe.matmul(bank[:, z * S:(z + 1) * S], w[:, i * P:(i + 1) * P], xnt[:, nxt, :],
                                            start=True, stop=True)
                        ins.then_inc(full[b], 1)
                    elif what == "v":
                        pe.matmul(bank[:], xnt[:, nxt, (i // 2) * P:(i // 2 + 1) * P],
                                  W["wv"][:, (i % 2) * 512:(i % 2 + 1) * 512], start=True, stop=True).then_inc(full[b], 1)
                    elif what == "max":
                        if i % 2 == 0:
                            pe.wait_ge(s["half"], half_t.add())
                        wait(pe, s["maxed"], maxed_t.add() - 2)
                        for t in range(NT):
                            ins = pe.matmul(Sb[i % 2][:, t * S:(t + 1) * S], qk16[rows(i), nxt, i // 2, 0, t * P:(t + 1) * P],
                                            qk16[rows(i), nxt, i // 2, 1, :], start=True, stop=True)
                        ins.then_inc(s["scores"], 1)
                    elif what == "turnmax":
                        pe.wait_ge(s["shifted"], shifted_t.add())
                        for t in range(NT):
                            ins = pe.transpose(bank[:].bitcast(BF16)[:, t * P:(t + 1) * P],
                                               parts[:, nxt, t].rearrange("p z r -> p (z r)"), K.ident16[:])
                        ins.then_inc(full[b], 1)
                    elif what == "score":
                        if i == 0:
                            for z in range(2):
                                wait(pe, drained[z], fill[z].value())
                        wait(pe, s["exps"], scored_t.add() - 2)
                        for t in range(NT):
                            at = Tb[i % 2][:, t * S:(t + 1) * S]
                            pe.matmul(at, qk[rows(i), par, i // 2, 1, t * P:(t + 1) * P], qk[rows(i), par, i // 2, 0, :],
                                      start=True, stop=False)
                            ins = pe.matmul(at, pick[rows(i), i, :], shift[rows(i), par, :], start=False, stop=True)
                        ins.then_inc(s["scored"], 1)
                    elif what == "value":
                        if i % 2 == 0:
                            wait(pe, s["divided"], o_t.add() - 2)
                        pe.wait_ge(s["exps"], exps_t.add())
                        for t in range(NT):
                            col = ((i % 2) * NT + t) * (D64 + 1)
                            for kt in range(NT):
                                ins = pe.matmul(Ob[i // 2 % 2][:, col:col + D64 + 1],
                                                pr[:, i % 2, kt * S + t * P:kt * S + (t + 1) * P], va[:, par, kt, i, :],
                                                start=(kt == 0), stop=(kt == NT - 1))
                        ins.then_inc(s["valued"], 1)
                    elif what == "attn":
                        if i == 0:
                            pe.wait_ge(s["divided"], divided_t.add(PAIRS))
                        for c in range(2):
                            for t in range(NT):
                                ins = pe.transpose(bank[:, (c * NT + t) * P:(c * NT + t + 1) * P],
                                                   att[:, nxt, t, 4 * i + 2 * c:4 * i + 2 * c + 2, :].rearrange("p h d -> p (h d)"),
                                                   K.ident[:])
                        ins.then_inc(full[b], 1)
                    elif what == "project":
                        for z in range(2):
                            wait(pe, drained[z], fill[z].value(1 if z == b else 0))
                        for t in range(NT):
                            for c in range(PAIRS):
                                ins = pe.matmul(bank[:, t * C:(t + 1) * C], att_t[:, c, t * P:(t + 1) * P], W["wo"][:, c, :],
                                                start=(c == 0), stop=(c == PAIRS - 1))
                        ins.then_inc(full[b], 1)

            pe.wait_ge(s["dve_set"], 1)
            batches(pe, tallies, step)

        @block.scalar
        def _(act):
            fill = fill_tallies()
            scored_t, valued_t = Tally(s["scored"], H), Tally(s["valued"], H)
            tallies = fill + [scored_t, valued_t]

            def step(n, par, do_a, do_b, do_e):
                nxt = 1 - par
                for what, i in wide_schedule(do_a, do_b, do_e):
                    b, filling = bank_of(fill, what, i)
                    if what == "norm":
                        for t in range(NT):
                            tile = bass.ds((n + 1) * NT + t, 1)
                            ins = act.activation(xn[:, nxt, t, :], K.X[:, tile, :].rearrange("p a c -> p (a c)"),
                                                 ACT.Identity, bias=K.shift[:, tile], scale=K.rstd[:, tile])
                        ins.then_inc(s["xn"], 1)
                        act.wait_ge(full[b], filling)
                        act.activation(xnt[:, nxt, :], Mb[b][:, 0:S], ACT.Copy).then_inc(drained[b], 1)
                    elif what == "qk":
                        act.wait_ge(full[b], filling)
                        act.activation(qk[:, nxt, i].rearrange("p z s -> p (z s)"), Mb[b][:], ACT.Copy).then_inc(drained[b], 1)
                    elif what == "score":
                        act.wait_ge(s["scored"], scored_t.add())
                        wait(act, s["valued"], valued_t.add() - 2)
                        act.activation(pr[:, i % 2, :], Tb[i % 2][:], ACT.Exp).then_inc(s["exps"], 1)

            stat_act(act)
            act.wait_ge(s["norm_ready"], 1)
            batches(act, tallies, step)

        @block.vector
        def _(dve):
            fill = fill_tallies()
            scores_t, maxed_t, valued_t = Tally(s["scores"], H), Tally(s["maxed"], H), Tally(s["valued"], H)
            own, divided_t = Chain(dve, s["dve_own"], 3 + PAIRS), Tally(s["divided"], PAIRS)
            biased_t, stats_t = Tally(s["biased"], 1), Tally(s["stats"], NT)
            tallies = fill + [scores_t, maxed_t, valued_t, own.t, divided_t, biased_t, stats_t]

            def step(n, par, do_a, do_b, do_e):
                nxt = 1 - par
                for what, i in wide_schedule(do_a, do_b, do_e):
                    b, filling = bank_of(fill, what, i)
                    if what == "v":
                        dve.wait_ge(full[b], filling)
                        dve.tensor_copy(va[:, nxt, i // 2, 8 * (i % 2):8 * (i % 2) + 8, 0:D64],
                                        Mb[b][:].rearrange("p (h d) -> p h d", d=D64)).then_inc(drained[b], 1)
                    elif what == "attn":
                        dve.wait_ge(full[b], filling)
                        dve.tensor_copy(att_t[:, 2 * i:2 * i + 2, :].rearrange("p c s -> p (c s)"), Mb[b][:]).then_inc(drained[b], 1)
                    elif what == "max":
                        dve.wait_ge(s["scores"], scores_t.add())
                        maxed_t.add()
                        dve.tensor_reduce(mx[:, nxt, :, i], Sb[i % 2][:].rearrange("p (t k) -> p t k", k=S), AX.X,
                                          ALU.max, negate=True).then_inc(s["maxed"], 1)
                    elif what == "split":
                        to = [parts[:, nxt, :, :, H * j:H * (j + 1)] for j in range(3)]
                        twice = [a.unsqueeze(2).to_broadcast([P, NT, 2, H]) for a in (mx[:, nxt], mrest[:])]
                        dve.wait_ge(s["maxed"], maxed_t.value())
                        own.done(dve.tensor_copy(to[0], twice[0]))
                        own.done(dve.tensor_tensor(mrest[:], mx[:, nxt], to[0][:, :, 0, :], ALU.subtract))
                        own.done(dve.tensor_copy(to[1], twice[1]))
                        dve.tensor_tensor(to[2], twice[1], to[1], ALU.subtract).then_inc(s["shifted"], 1)
                    elif what == "turnmax":
                        dve.wait_ge(full[b], filling)
                        dve.tensor_copy(shift[:, nxt, :], Mb[b][:].bitcast(BF16)[:, 0:S]).then_inc(drained[b], 1)
                    elif what == "divide":
                        dve.wait_ge(s["valued"], valued_t.add(2))
                        o = Ob[i % 2][:, 0:2 * NT * (D64 + 1)].rearrange("p (z t e) -> p t z e", z=2, t=NT)
                        r = rc[:].rearrange("p (t z) -> p t z", t=NT)
                        wait(dve, s["divided"], divided_t.value())
                        own.done(dve.reciprocal(r, o[:, :, :, D64]))
                        divided_t.add()
                        dve.tensor_tensor(att[:, par, :, 2 * i:2 * i + 2, :], o[:, :, :, 0:D64],
                                          r.unsqueeze(3).to_broadcast([P, NT, 2, D64]), ALU.mult).then_inc(s["divided"], 1)
                    elif what == "project":
                        dve.wait_ge(s["biased"], biased_t.add())
                        dve.wait_ge(full[b], filling)
                        x = K.X[:, bass.ds((n - 1) * NT, NT), :]
                        dve.tensor_tensor(x, x, Mb[b][:, 0:NT * C].rearrange("p (t c) -> p t c", c=C),
                                          ALU.add).then_inc(drained[b], 1)
                        dve.wait_ge(drained[b], filling)
                        for t in range(NT):
                            tile = bass.ds((n - 1) * NT + t, 1)
                            dve.bn_stats(K.moments[:, tile, :].rearrange("p a m -> p (a m)"),
                                         K.X[:, tile, :].rearrange("p a c -> p (a c)")).then_inc(s["stats"], 1)
                        stats_t.add(NT)

            stat_dve(dve)
            dve.wait_ge(s["pool_set"], POOL_SETS)
            dve.tensor_scalar(W["wq"], W["wq"], float(D64) ** -0.5, None, ALU.mult).then_inc(s["dve_set"], 1)
            batches(dve, tallies, step)
            dve.wait_ge(s["stats"], stats_t.value())

        @block.gpsimd
        def _(pool):
            fill = fill_tallies()
            xn_t = Tally(s["xn"], 1)
            tallies = fill + [xn_t]

            def step(n, par, do_a, do_b, do_e):
                nxt = 1 - par
                for what, i in wide_schedule(do_a, do_b, do_e):
                    b, filling = bank_of(fill, what, i)
                    if what == "norm":
                        pool.wait_ge(s["xn"], xn_t.add())
                        x = K.X[:, bass.ds((n + 1) * NT, NT), :]
                        pool.tensor_tensor(x, x, W["bias"].unsqueeze(1).to_broadcast([P, NT, C]), ALU.add).then_inc(s["biased"], 1)
                    elif what == "qk":
                        wait(pool, drained[b], filling)
                        pool.sem_inc(s["waited"], 1)
                        pool.tensor_copy(qk16[:, nxt, i], qk[:, nxt, i]).then_inc(s["half"], 1)

            set_ = s["pool_set"]
            pool.memset(va[:, :, :, :, D64:D64 + 1], 1.0).then_inc(set_, 1)
            pool.memset(parts[:], 0.0).then_inc(set_, 1)
            pool.memset(pick[:], 0.0).then_inc(set_, 1)
            pool.wait_ge(set_, 3)
            for z in range(2):
                for j in range(3):
                    base = -(64 * z + H * j)
                    ins = pool.affine_select(out=pick[:], in_=pick[:], compare_op=ALU.not_equal, fill=1.0, base=base,
                                             pattern=[[-1, H], [0, P]], channel_multiplier=1)
                    if z * 3 + j < 5:
                        ins.then_inc(s["pool_own"], 1)
                        pool.wait_ge(s["pool_own"], z * 3 + j + 1)
            ins.then_inc(set_, 3)
            batches(pool, tallies, step)



class Kept:
    pass


LAYERS = ["wide", "experts", "slope", "experts", "rope", "group", "recurrent", "group"]


def program(nc, A, out):
    K = Kept()
    K.REG = 5
    K.narrow_sets = {"slope": 6 + NT * 2, "rope": 5, "group": 5}
    ctx = ExitStack()
    with ctx:
        def sb(n, shape, dt=F32):
            return ctx.enter_context(nc.sbuf_tensor(n, shape, dt))

        K.X = sb("x", [P, TILES, C])
        K.moments = sb("moments", [P, TILES, 6])
        K.mean, K.spread, K.var = sb("mean", [P, TILES]), sb("spread", [P, TILES]), sb("var", [P, TILES])
        K.rstd, K.shift = sb("rstd", [P, TILES]), sb("shift", [P, TILES])
        K.ident, K.ident16 = sb("ident", [P, P]), sb("ident16", [P, P], BF16)
        K.causal_kq, K.causal_qk = sb("causal_kq", [P, P], BF16), sb("causal_qk", [P, P], BF16)
        K.position_i, K.position = sb("position_i", [P, NT], I32), sb("position", [P, NT])
        K.own_head = sb("own_head", [P, K.REG * H])
        K.not_first = sb("not_first", [STACK, K.REG * H], BF16)
        K.mask_q, K.mask_k = sb("mask_q", [P, TILES, 2], BF16), sb("mask_k", [P, TILES, 2], BF16)
        banks = [ctx.enter_context(nc.psum_tensor(f"bank{n}", [P, 512], F32)) for n in range(8)]
        K.Sb, K.Tb, K.Ob, K.Mb = banks[0:2], banks[2:4], banks[4:6], banks[6:8]
        K.banks = banks
        K.x_in = A["L0_attn_a_x"].rearrange("b (t p) c -> p (b t) c", p=P)

        loads = []

        def weight(n, shape, src):
            t = sb(n, shape)
            loads.append((t[:], src))
            return t

        def row(n, src, width):
            return weight(n, [P, width], src.partition_broadcast(P))

        K.slopes = row("slopes", A["L0_attn_b_m"].rearrange("h a b -> (h a b)"), H)
        w_slope = weight("w_slope", [P, 3 * C], A["L0_attn_b_W_kqv"])
        W_slope = {"qk": w_slope[:, 0:2 * C], "v": w_slope[:, 2 * C:3 * C], "k_at": 0, "q_at": C, "scale": (w_slope[:, C:2 * C], float(C) ** -0.5)}

        w_a = sb("w_lowrank", [P, 96])
        loads.append((w_a[:, 0:64], A["L1_attn_a_Wqa"]))
        loads.append((w_a[:, 64:96], A["L1_attn_a_Wkva"]))
        w_b = sb("w_lowrank_out", [96, C])
        loads.append((w_b[0:64, :], A["L1_attn_a_Wqb"]))
        loads.append((w_b[64:96, 0:64], A["L1_attn_a_Wkvb"]))
        K.cos, K.sin = weight("cos", [P, NT, 160], A["cos"]), weight("sin", [P, NT, 160], A["sin"])
        w_rope_out = weight("w_rope_out", [P, C], A["L1_attn_a_Wout"])
        b_rope = row("b_rope", A["L1_attn_a_bout"], C)
        W_rope = {"a": w_a[:], "qb": w_b[0:64, :], "kvb": w_b[64:96, 0:64], "out": w_rope_out[:], "bias": b_rope[:]}

        w_group = weight("w_group", [P, 3 * C], A["L1_ffn_W_qkv"])
        w_group_out = weight("w_group_out", [P, C], A["L1_ffn_W_proj"])
        b_group = row("b_group", A["L1_ffn_b_proj"], C)
        K.guide = row("guide", A["L1_ffn_g_info"][0, 0, :], C)
        W_group = {"qk": w_group[:, 0:2 * C], "v": w_group[:, 2 * C:3 * C], "q_at": 0, "k_at": C, "q": w_group[:, 0:C], "k": w_group[:, C:2 * C],
                   "out": w_group_out[:], "bias": b_group[:], "scale": (w_group[:, 0:C], float(D8) ** -0.5)}

        w_gate = weight("w_gate", [P, E8], A["L0_ffn_gate_w"])
        w1 = weight("w1", [P, E8, HID], A["L0_ffn_w1"].rearrange("e c h -> c e h"))
        w2 = weight("w2", [P, E8, HC, C], A["L0_ffn_w2"].rearrange("e (k p) c -> p e k c", p=P))
        W_experts = {"gate": w_gate[:], "w1": w1, "w2": w2}

        w_q, w_k = weight("w_q", [P, H * D64], A["L0_attn_a_Wq"]), weight("w_k", [P, H * D64], A["L0_attn_a_Wk"])
        w_v = weight("w_v", [P, H * D64], A["L0_attn_a_Wv"])
        w_o = weight("w_o", [P, PAIRS, C], A["L0_attn_a_Wo"].rearrange("(k p) c -> p k c", p=P))
        b_o = row("b_o", A["L0_attn_a_bo"], C)
        W_wide = {"wq": w_q[:], "wk": w_k[:], "wv": w_v[:], "wo": w_o, "bias": b_o[:]}

        w_ra, w_rx = weight("w_ra", [P, C], A["L1_attn_b_Wa"]), weight("w_rx", [P, C], A["L1_attn_b_Wx"])
        columns = sb("columns", [P, 3])
        for n, key in enumerate(("L1_attn_b_ba", "L1_attn_b_bx", "L1_attn_b_Lam")):
            loads.append((columns[:, n:n + 1], A[key].unsqueeze(1)))
        W_recurrent = {"wa": w_ra[:], "wx": w_rx[:], "ba": columns[:, 0:1], "bx": columns[:, 1:2], "lam": columns[:, 2:3]}

        load(nc, K, loads)
        for n, layer in enumerate(LAYERS):
            name = f"l{n}_{layer}"
            if layer == "slope":
                narrow_attention(nc, K, "slope", name, W_slope)
            if layer == "rope":
                narrow_attention(nc, K, "rope", name, W_rope)
            if layer == "group":
                groups(nc, K, name, W_group)
                narrow_attention(nc, K, "group", name, W_group)
                W_group.pop("scale", None)
            if layer == "recurrent":
                recurrent(nc, K, name, W_recurrent)
            if layer == "experts":
                experts(nc, K, name, W_experts)
            if layer == "wide":
                wide_attention(nc, K, name, W_wide)

        with ExitStack() as last:
            stored = nc.alloc_semaphore(name="stored")
            block = last.enter_context(nc.Block("store"))

            @block.sync
            def _(sp):
                sp.dma_start(out.rearrange("b (t p) c -> p (b t) c", p=P), K.X[:]).then_inc(stored, 16)
                sp.wait_ge(stored, 16)


def kernel(**inputs):
    import numpy as np
    import concourse.bacc as bacc
    from concourse.bass_utils import run_bass_kernel_spmd

    nc = bacc.Bacc("TRN2", target_bir_lowering=False, num_devices=1)
    arrays = {k: np.ascontiguousarray(v) for k, v in inputs.items()}
    arrays["L1_attn_a_Wqb"] = np.ascontiguousarray(
        arrays["L1_attn_a_Wqb"].reshape(64, H, 4, 2).transpose(0, 3, 1, 2).reshape(64, C))
    kv = arrays["L1_attn_a_Wkvb"].reshape(32, 4, 4, 2, 2)
    arrays["L1_attn_a_Wkvb"] = np.ascontiguousarray(np.concatenate(
        [kv[..., 0].transpose(0, 3, 1, 2).reshape(32, 32), kv[..., 1].reshape(32, 32)], axis=1))
    inv = (1.0 / 10000.0 ** (np.arange(0, D8, 2, dtype=np.float32) / D8)).astype(np.float32)
    angle = np.outer(np.arange(S, dtype=np.float32), inv).astype(np.float32)
    scale = np.repeat(np.float32([D8 ** -0.5, 1.0]), [H, 4])
    cos = scale[:, None] * np.cos(angle)[:, None, :]
    sin = scale[:, None] * np.sin(angle)[:, None, :]
    tables = {"cos": np.stack([cos, cos], 1), "sin": np.stack([-sin, sin], 1)}
    for k, v in tables.items():
        arrays[k] = np.ascontiguousarray(v.reshape(NT, P, 160).transpose(1, 0, 2).astype(np.float32))
    A = {k: nc.dram_tensor(f"in_{k}_dram", v.shape, mybir.dt.from_np(v.dtype), kind="ExternalInput").ap()
         for k, v in arrays.items()}
    out = nc.dram_tensor("out_0_dram", arrays["L0_attn_a_x"].shape, F32, kind="ExternalOutput").ap()
    program(nc, A, out)
    r = run_bass_kernel_spmd(nc, [{f"in_{k}_dram": v for k, v in arrays.items()}], core_ids=[0])
    return r.results[0]["out_0_dram"]
```
